# Optimizing a Trainium2 kernel written in Bass

```python
import numpy as np
import jax
import jax.numpy as jnp

def _softmax(x, axis=-1):
    return jax.nn.softmax(x, axis=axis)
def _gelu(x):
    return jax.nn.gelu(x, approximate=True)
def _silu(x):
    return jax.nn.silu(x)
def _sigmoid(x):
    return jax.nn.sigmoid(x)
def _layernorm(x, axis=-1, eps=1e-5):
    m = jnp.mean(x, axis=axis, keepdims=True)
    v = jnp.var(x, axis=axis, keepdims=True)
    return (x - m) / jnp.sqrt(v + eps)
def _scatter_add(tgt, idx, src, axis=0):
    return tgt.at[idx].add(src)
def _segment_sum(src, seg, n):
    return jax.ops.segment_sum(src, seg, n)

kernel_name = 'mk_adj_seq_d2_adj_128_4e14c1'

def setup_inputs(seed: int = 0):
    np.random.seed(seed)
    _w = jnp.asarray
    def _rec_inputs():
        import jax
        import jax.numpy as jnp
        _gk = jax.random.key(seed)
        x = -0.000929 + 1 * jax.random.normal(jax.random.fold_in(_gk, 1), (8, 2048, 128), jnp.float32)
        _a = jax.random.bernoulli(jax.random.fold_in(_gk, 2), 0.00195312, (8, 2048, 2048))
        _a = jnp.logical_or(_a, jnp.swapaxes(_a, -1, -2))
        _a = jnp.logical_or(_a, jnp.eye(2048, dtype=bool))
        _af = _a.astype(jnp.float32)
        _af = _af * jax.random.uniform(jax.random.fold_in(_gk, 3), (8, 2048, 2048), jnp.float32, 0.05, 1)
        adj = _af
        return x, adj
    x, adj = _rec_inputs()
    def _L0_gnn_setup():
        import jax, jax.numpy as jnp
        import numpy as np
        B, N, F = (4, 2048, 128)
        EPS = 1e-06

        def _normalize_adj(adj):
            deg = jnp.sum(adj, axis=-1)
            dinv = jnp.power(deg + EPS, -0.5)
            return dinv[:, :, None] * adj * dinv[:, None, :]

        def _gcn(x, adj_norm, W, b, act):
            z = jnp.einsum('bij,bjf->bif', adj_norm, x)
            z = jnp.einsum('bif,fo->bio', z, W) + b
            return act(z) if act is not None else z
        key = jax.random.key(seed)
        ks = jax.random.split(key, 8)
        x = jax.random.normal(ks[0], (B, N, F), dtype=jnp.float32)
        adj = jax.random.uniform(ks[1], (B, N, N), dtype=jnp.float32)
        limit = float(np.sqrt(6.0 / (F + F)))
        W1 = jax.random.uniform(ks[2], (F, F), minval=-limit, maxval=limit, dtype=jnp.float32)
        W2 = jax.random.uniform(ks[3], (F, F), minval=-limit, maxval=limit, dtype=jnp.float32)
        W3 = jax.random.uniform(ks[4], (F, F), minval=-limit, maxval=limit, dtype=jnp.float32)
        b1 = jnp.zeros((F,), dtype=jnp.float32)
        b2 = jnp.zeros((F,), dtype=jnp.float32)
        b3 = jnp.zeros((F,), dtype=jnp.float32)
        return {'x': x, 'adj': adj, 'W1': W1, 'b1': b1, 'W2': W2, 'b2': b2, 'W3': W3, 'b3': b3}
    _L0_gnn_all = _L0_gnn_setup()
    _L0_gnn_in = {k: v for k, v in _L0_gnn_all.items() if k in ('W1', 'b1', 'W2', 'b2', 'W3', 'b3', )}
    del _L0_gnn_all

    def _L1_gnn_setup():
        import jax, jax.numpy as jnp
        import numpy as np
        B, N, D = (8, 2048, 128)
        NEG = -9000000000000000.0
        key = jax.random.key(seed)
        k = jax.random.split(key, 7)
        x = jax.random.normal(k[0], (B, N, D), dtype=jnp.float32)
        adj = (jax.random.uniform(k[1], (B, N, N)) < 0.1).astype(jnp.float32)
        adj = jnp.maximum(adj, jnp.eye(N, dtype=jnp.float32)[None])
        s = 1.0 / np.sqrt(D)
        W_w = jax.random.normal(k[2], (D, D), dtype=jnp.float32) * s
        W_b = jax.random.normal(k[3], (D,), dtype=jnp.float32) * s
        A = jax.random.normal(k[4], (D, D), dtype=jnp.float32) * s
        gate_w = jax.random.normal(k[5], (2 * D, 1), dtype=jnp.float32) * (1.0 / np.sqrt(2 * D))
        gate_b = jax.random.normal(k[6], (1,), dtype=jnp.float32)
        return {'x': x, 'adj': adj, 'W_w': W_w, 'W_b': W_b, 'A': A, 'gate_w': gate_w, 'gate_b': gate_b}
    _L1_gnn_all = _L1_gnn_setup()
    _L1_gnn_in = {k: v for k, v in _L1_gnn_all.items() if k in ('W_w', 'W_b', 'A', 'gate_w', 'gate_b', )}
    del _L1_gnn_all

    return {
        "x": x,
        "adj": adj,
        "L0_gnn_W1": _L0_gnn_in["W1"],
        "L0_gnn_b1": _L0_gnn_in["b1"],
        "L0_gnn_W2": _L0_gnn_in["W2"],
        "L0_gnn_b2": _L0_gnn_in["b2"],
        "L0_gnn_W3": _L0_gnn_in["W3"],
        "L0_gnn_b3": _L0_gnn_in["b3"],
        "L1_gnn_W_w": _L1_gnn_in["W_w"],
        "L1_gnn_W_b": _L1_gnn_in["W_b"],
        "L1_gnn_A": _L1_gnn_in["A"],
        "L1_gnn_gate_w": _L1_gnn_in["gate_w"],
        "L1_gnn_gate_b": _L1_gnn_in["gate_b"],
    }

def reference(x, adj, L0_gnn_W1, L0_gnn_b1, L0_gnn_W2, L0_gnn_b2, L0_gnn_W3, L0_gnn_b3, L1_gnn_W_w, L1_gnn_W_b, L1_gnn_A, L1_gnn_gate_w, L1_gnn_gate_b):
    import jax
    import jax.numpy as jnp
    def _L0_gnn_ref(x, adj, W1, b1, W2, b2, W3, b3):
        import jax, jax.numpy as jnp
        import numpy as np
        B, N, F = (4, 2048, 128)
        EPS = 1e-06

        def _normalize_adj(adj):
            deg = jnp.sum(adj, axis=-1)
            dinv = jnp.power(deg + EPS, -0.5)
            return dinv[:, :, None] * adj * dinv[:, None, :]

        def _gcn(x, adj_norm, W, b, act):
            z = jnp.einsum('bij,bjf->bif', adj_norm, x)
            z = jnp.einsum('bif,fo->bio', z, W) + b
            return act(z) if act is not None else z
        adj_norm = _normalize_adj(adj)
        h = _gcn(x, adj_norm, W1, b1, jax.nn.relu) + x
        h = _gcn(h, adj_norm, W2, b2, jax.nn.relu) + h
        h = _gcn(h, adj_norm, W3, b3, None) + h
        return h

    def _L1_gnn_ref(x, adj, W_w, W_b, A, gate_w, gate_b):
        import jax, jax.numpy as jnp
        import numpy as np
        B, N, D = (8, 2048, 128)
        NEG = -9000000000000000.0
        h = jnp.einsum('bnd,ed->bne', x, W_w) + W_b
        e = jnp.einsum('bjl,bkl->bjk', h @ A, h)
        e = e + jnp.swapaxes(e, 1, 2)
        attention = jnp.where(adj > 0, e, jnp.float32(NEG))
        attention = jax.nn.softmax(attention, axis=1)
        attention = attention * adj
        h_prime = jax.nn.relu(jnp.einsum('bij,bjk->bik', attention, h))
        coeff = jnp.concatenate([x, h_prime], axis=-1) @ gate_w + gate_b
        return coeff * x + (1.0 - coeff) * h_prime

    x = _L0_gnn_ref(x, adj, L0_gnn_W1, L0_gnn_b1, L0_gnn_W2, L0_gnn_b2, L0_gnn_W3, L0_gnn_b3)
    x = _L1_gnn_ref(x, adj, L1_gnn_W_w, L1_gnn_W_b, L1_gnn_A, L1_gnn_gate_w, L1_gnn_gate_b)
    return x


_drawn_inputs = setup_inputs


def setup_inputs(seed=0):
    import zlib

    import numpy as np

    out = dict(_drawn_inputs(seed))
    spreads = {'L0_gnn_b1': (0.0, 0.1), 'L0_gnn_b2': (0.0, 0.1), 'L0_gnn_b3': (0.0, 0.1)}
    factors = {}
    for name, (base, spread) in spreads.items():
        noise = np.random.default_rng([zlib.crc32(name.encode()), seed]).standard_normal(out[name].shape)
        drawn = base * np.exp(spread * noise) if base else spread * noise
        out[name] = jnp.asarray(drawn.astype(out[name].dtype))
    for name, factor in factors.items():
        out[name] = (out[name] * factor).astype(out[name].dtype)
    return out
```

```python
from contextlib import ExitStack

import concourse.bass as bass
from concourse import mybir

ALU = mybir.AluOpType
ACT = mybir.ActivationFunctionType
F32 = mybir.dt.float32
F32R = mybir.dt.float32r
BF16 = mybir.dt.bfloat16
AX_X = mybir.AxisListType.X

P = 128
N = 2048
Q = 4
C = 32
T = N // P
G = 4
TG = T // G
CH = N // G
L = 3
EPS = 1e-6
NEG = -9000000000000000.0
LOWEST = -3.4e38

NU = L * T * 2
HALF = N // 2
RINGU = 3
ROWS = 256
NB = ROWS // C
NV = (N // ROWS) * G
NSTG = 3
RINGC = 3
DEG_UNITS = 2 * T


def unit_order():
    order = []
    for layer in range(L):
        order += [(layer, t, h) for t in range(T - 2) for h in range(2)]
        order += [(layer, t, h) for h in range(2) for t in (T - 2, T - 1)]
    return order


UNITS = unit_order()
ON_POOL = [u % 4 == 1 for u in range(NU)]
POOL_PER_GRAPH = sum(ON_POOL)
DVE_PER_GRAPH = NU - POOL_PER_GRAPH


def lo_count(u, pool):
    return sum(1 for v in range(u + 1) if ON_POOL[v] == pool)


def last_unit(layer, t):
    return max(u for u, (l, s, _) in enumerate(UNITS) if l == layer and s == t)


def chunk_done(layer, g):
    return max(u for u, (l, _, h) in enumerate(UNITS) if l == layer and h == g // 2)


def stage_count(v, slot):
    return sum(1 for w in range(v + 1) if w % NSTG == slot)


STAGES = [stage_count(NV - 1, s) for s in range(NSTG)]


def gnn_kernel(nc, x, adj, W1, b1, W2, b2, W3, b3, W_w, W_b, A, gate_w, gate_b, out):
    B = x.shape[0]
    nc.disable_value_cache = True

    with ExitStack() as ctx:
        def sem(name):
            return ctx.enter_context(nc.semaphore(name))

        base = (nc.sbuf_base + 63) // 64 * 64
        top = [base]

        def place(nbytes):
            at = top[0]
            top[0] += (nbytes + 31) // 32 * 32
            assert top[0] <= nc.sbuf_usable_end
            return at

        def sb(name, shape, dt, offset):
            return nc.alloc_sbuf_tensor_at(name, shape, dt, offset=offset)

        adj_t = sb("adj_t", [P, T, N], F32, place(T * N * 4))
        blk = [place(N * 4) for _ in range(4)]
        ring0 = place(RINGC * N * 4)
        feat = sb("feat", [P, T, P], F32, blk[0])
        deg_rows = sb("deg_rows", [P, 2, HALF], F32, blk[1])
        xs_hi = sb("xs_hi", [P, T, P], F32R, blk[2])
        xs_lo = sb("xs_lo", [P, T, P], F32R, blk[3])
        ut_lo = sb("ut_lo", [P, T, P], F32R, blk[0])
        ht_hi = sb("ht_hi", [P, N], F32R, blk[1])
        ht_lo = sb("ht_lo", [P, N], F32R, blk[2])
        ut_hi = sb("ut_hi", [P, T, P], F32R, blk[3])
        gathered = sb("gathered", [P, T, P], F32, blk[1])
        a_hi = [sb(f"a_hi{s}", [P, Q, 2 * P], F32R, ring0 + s * N * 4) for s in range(RINGU)]
        a_lo = [sb(f"a_lo{s}", [P, Q, 2 * P], F32R, ring0 + s * N * 4 + HALF * 4) for s in range(RINGU)]
        prob = [sb(f"prob{s}", [P, N], F32, ring0 + s * N * 4) for s in range(RINGC)]
        x4_t = sb("x4_t", [P, T, P], F32, ring0 + 1 * N * 4)
        h_rows = sb("h_rows", [P, T, P], F32, ring0 + 2 * N * 4)
        stage = [sb(f"stage{s}", [P, NB, P], F32, place(NB * P * 4)) for s in range(NSTG)]
        pair0, pair1 = place(CH * 4), place(CH * 4)
        z_sb = [sb("z_sb0", [P, CH], F32, pair0), sb("z_sb1", [P, CH], F32, pair1)]
        x4_back = [sb("x4_back0", [P, CH], F32, pair0), sb("x4_back1", [P, CH], F32, pair1)]
        mask = sb("mask", [P, HALF], BF16, pair0)
        h_in = [sb(f"h_in{s}", [P, P], F32, place(P * 4)) for s in range(2)]
        h_norm = [sb(f"h_norm{s}", [P, P], F32, place(P * 4)) for s in range(2)]
        w_sb = sb("w_sb", [P, L, P], F32, place(L * P * 4))
        ww_t = sb("ww_t", [P, P], F32, place(P * 4))
        sw_t = sb("sw_t", [P, P], F32, place(P * 4))
        ident = sb("ident", [P, P], F32, place(P * 4))
        bias = sb("bias", [P, L + 1, P], F32, place((L + 1) * P * 4))
        columns = sb("columns", [P, 15 + 8 * T], F32, place((15 + 8 * T) * 4))
        taken = [0]

        def cols(n):
            taken[0] += n
            return columns[:, taken[0] - n:taken[0]]

        wb_col = cols(2)
        gate = cols(2)
        gb = cols(1)
        deg_part = cols(2 * T).rearrange("p (t h) -> p t h", h=2)
        deg, root, newton, dinv = cols(T), cols(T), cols(T), cols(T)
        top_half, top_full, neg_top, total, inv_total = ([cols(1), cols(1)] for _ in range(5))
        coef_x, coef = cols(T), cols(T)
        raw_ww = sb("raw_ww", [P, P], F32, ring0)
        raw_a = sb("raw_a", [P, P], F32, ring0 + P * 4)
        a_sym = sb("a_sym", [P, P], F32, ring0 + 2 * P * 4)

        ps_z = [ctx.enter_context(nc.psum_tensor(f"ps_z{g}", [P, CH], F32)) for g in range(G)]
        ps_e = ctx.enter_context(nc.psum_tensor("ps_e", [P, N], F32))

        def bank(g):
            return ps_e[:, g * CH:(g + 1) * CH]

        x4_dram = nc.dram_tensor("x4_dram", (P, N), F32, kind="Internal").ap()
        h_dram = nc.dram_tensor("h_dram", (P, N), F32, kind="Internal").ap()

        s_const = sem("s_const")
        s_ident0, s_ident = sem("s_ident0"), sem("s_ident")
        s_wt, s_sym, s_wc, s_sw, s_swc = sem("s_wt"), sem("s_sym"), sem("s_wc"), sem("s_sw"), sem("s_swc")
        s_x = sem("s_x")
        s_rows = [sem(f"s_rows{s}") for s in range(2)]
        s_deg = sem("s_deg")
        s_dsum, s_root, s_newton, s_dinv = sem("s_dsum"), sem("s_root"), sem("s_newton"), sem("s_dinv")
        s_stage = [sem(f"s_stage{s}") for s in range(NSTG)]
        s_turned = sem("s_turned")
        s_hi, s_lo_dve, s_lo_pool = sem("s_hi"), sem("s_lo_dve"), sem("s_lo_pool")
        s_unit = sem("s_unit")
        s_zsb, s_zw, s_affine, s_h = sem("s_zsb"), sem("s_zw"), sem("s_affine"), sem("s_h")
        s_xhi, s_xlo = sem("s_xhi"), sem("s_xlo")
        s_spill = [sem(f"s_spill{g}") for g in range(G)]
        s_xt, s_xtc = sem("s_xt"), sem("s_xtc")
        s_ht, s_hthi, s_htlo = sem("s_ht"), sem("s_hthi"), sem("s_htlo")
        s_ut, s_uthi, s_utlo = sem("s_ut"), sem("s_uthi"), sem("s_utlo")
        s_hr, s_hrc = sem("s_hr"), sem("s_hrc")
        s_hspill = sem("s_hspill")
        s_cx, s_cxc = sem("s_cx"), sem("s_cxc")
        s_e = sem("s_e")
        s_mask, s_top, s_neg = sem("s_mask"), sem("s_top"), sem("s_neg")
        s_exp, s_prob = sem("s_exp"), sem("s_prob")
        s_inv, s_hnorm = sem("s_inv"), sem("s_hnorm")
        s_hin = [sem(f"s_hin{s}") for s in range(2)]
        s_pv = sem("s_pv")
        s_rel, s_cg, s_coef0, s_coef, s_gt = (sem("s_rel"), sem("s_cg"), sem("s_coef0"),
                                              sem("s_coef"), sem("s_gt"))
        s_back = [sem(f"s_back{s}") for s in range(2)]
        s_diff, s_res = sem("s_diff"), sem("s_res")
        s_out = sem("s_out")

        s_met_dve, s_met_sp = sem("s_met_dve"), sem("s_met_sp")

        def natural(ap, g):
            return ap.rearrange("p (q g x) -> p g q x", q=Q, g=G)[:, g]

        def chunk_of_unit(buf, g):
            return buf[:, :, (g % 2) * P:(g % 2 + 1) * P]

        def half_columns(t, h):
            return adj_t[:, t].rearrange("p (q h x) -> p h q x", q=Q, h=2)[:, h]

        def by_tile(ap):
            return ap.rearrange("p (q s c) -> p q s c", q=Q, s=TG)

        def tile_major(ap):
            return ap.rearrange("p (s q c) -> p q s c", q=Q, s=TG)

        def by_quadrant(ap):
            return ap.rearrange("p (q x) -> p q x", q=Q)

        def tiles(buf, g):
            return buf[:, g * TG:(g + 1) * TG].rearrange("p s f -> p (s f)")

        def node_rows(dram, quadrant, t0, t1):
            per = N // Q
            return dram[quadrant * per + t0 * C:quadrant * per + t1 * C].rearrange("(t c) f -> c t f", c=C)

        bias_in = [b1, b2, b3, W_b]
        N_CONST = 5 + len(bias_in) + 4

        def settle(eng, passed):
            eng.sem_inc(passed, 1)

        def load_x(sp, b):
            for q in range(Q):
                sp.dma_start(feat[q * C:(q + 1) * C], node_rows(x[b], q, 0, T)).then_inc(s_x, 16)

        def load_rows(sp, b, k, first=False):
            for d in range(DEG_UNITS):
                if d >= 2 or not first:
                    sp.wait_ge(s_deg, DEG_UNITS * k + max(d - 1, 0))
                t, h = d // 2, d % 2
                for q in range(Q):
                    row = q * (N // Q) + t * C
                    sp.dma_start(deg_rows[q * C:(q + 1) * C, d % 2],
                                 adj[b, row:row + C, h * HALF:(h + 1) * HALF]).then_inc(s_rows[d % 2], 16)

        def load_stage(sp, b, k, v, first=False):
            if v >= NSTG or not first:
                sp.wait_ge(s_turned, NV * k + max(v - NSTG + 1, 0))
            J, r = v // (N // ROWS), v % (N // ROWS)
            for q in range(Q):
                col = q * (N // Q) + J * P
                src = adj[b, r * ROWS:(r + 1) * ROWS, col:col + P].rearrange("(n c) j -> c n j", c=C)
                sp.dma_start(stage[v % NSTG][q * C:(q + 1) * C], src).then_inc(s_stage[v % NSTG], 16)

        def sync_graph(sp, b, more):
            if more:
                load_rows(sp, b + 1, b + 1)
                for v in range(NSTG):
                    load_stage(sp, b + 1, b + 1, v)
            for g in range(G):
                sp.wait_ge(s_h, 12 * b + 2 * G + g + 1)
                sp.dma_start(x4_dram[:, g * CH:(g + 1) * CH], tiles(feat, g)).then_inc(s_spill[g], 16)
            sp.wait_ge(s_hrc, G * b + G)
            sp.dma_start(h_dram, h_rows[:].rearrange("p t f -> p (t f)")).then_inc(s_hspill, 16)
            sp.wait_ge(s_hspill, 16 * b + 16)
            if more:
                for v in range(NSTG, 8):
                    load_stage(sp, b + 1, b + 1, v)
                for v in range(8, 27):
                    load_stage(sp, b + 1, b + 1, v)
                sp.wait_ge(s_e, 2 * T * b + 2 * T)
                load_x(sp, b + 1)
                for v in range(27, NV):
                    load_stage(sp, b + 1, b + 1, v)
            for g in range(G):
                sp.wait_ge(s_spill[g], 16 * b + 16)
                if g == 0:
                    sp.wait_ge(s_top, 2 * T * b + 2 * T)
                if g >= 2:
                    sp.wait_ge(s_diff, G * b + g - 1)
                sp.dma_start(x4_back[g % 2][:], x4_dram[:, g * CH:(g + 1) * CH]).then_inc(s_back[g % 2], 16)
            for g in range(G):
                sp.wait_ge(s_res, G * b + g + 1)
                for q in range(Q):
                    sp.dma_start(node_rows(out[b], q, g * TG, (g + 1) * TG),
                                 gathered[q * C:(q + 1) * C, g * TG:(g + 1) * TG]).then_inc(s_out, 16)
            sp.wait_ge(s_out, 16 * G * Q * b + 16 * G * Q)
            settle(sp, s_met_sp)

        def sum_rows(act, k, d):
            act.wait_ge(s_rows[d % 2], 16 * Q * T * k + 16 * Q * (d // 2 + 1))
            nc.scalar.activation(deg_rows[:, d % 2], deg_rows[:, d % 2], ACT.Copy,
                                 accum_out=deg_part[:, d // 2, d % 2:d % 2 + 1]).then_inc(s_deg, 1)

        def degree_root(act, k):
            act.wait_ge(s_dsum, k + 1)
            nc.scalar.activation(root[:], deg[:], ACT.Sqrt).then_inc(s_root, 1)

        def split_x(act, b, layer, g):
            if layer == 0:
                act.wait_ge(s_x, 16 * Q * b + 16 * Q)
                act.wait_ge(s_dinv, b + 1)
            else:
                act.wait_ge(s_h, 12 * b + (layer - 1) * G + g + 1)
                act.wait_ge(s_unit, NU * b + last_unit(layer - 1, g * TG + TG - 1) + 1)
            for t in range(g * TG, (g + 1) * TG):
                last = nc.scalar.activation(xs_hi[:, t], feat[:, t], ACT.Copy, scale=dinv[:, t:t + 1])
            last.then_inc(s_xhi, 1)

        def make_hi(act, b, u):
            layer, t, h = UNITS[u]
            if u >= RINGU:
                act.wait_ge(s_unit, NU * b + u - RINGU + 1)
            if layer == 0:
                act.wait_ge(s_turned, NV * b + 8 * (t // TG) + 8)
            nc.scalar.activation(a_hi[u % RINGU][:], half_columns(t, h), ACT.Copy).then_inc(s_hi, 1)

        def move_z(act, b, layer, g):
            i = layer * G + g
            act.wait_ge(s_unit, NU * b + chunk_done(layer, g) + 1)
            if i >= 2:
                act.wait_ge(s_zw, 12 * b + i - 1)
            nc.scalar.activation(tile_major(z_sb[g % 2][:]), by_tile(ps_z[g][:]), ACT.Copy).then_inc(s_zsb, 1)

        def scalar_graph(act, b, more):
            for g in range(G):
                split_x(act, b, 0, g)
            summed = 0
            for u in range(NU):
                make_hi(act, b, u)
                layer, t, h = UNITS[u]
                if more and u % 3 == 2:
                    sum_rows(act, b + 1, summed)
                    summed += 1
                for g in range(G):
                    if chunk_done(layer, g) + 1 == u:
                        pass
                if u == chunk_done(layer, 0) + 2 or u == chunk_done(layer, 2):
                    first = 0 if u == chunk_done(layer, 0) + 2 else 2
                    if first == 2:
                        for g in range(2):
                            pass
                if u % (NU // L) == NU // L - 1:
                    for g in range(G):
                        move_z(act, b, layer, g)
                    if layer < L - 1:
                        for g in range(G):
                            split_x(act, b, layer + 1, g)
            for g in range(G):
                act.wait_ge(s_xt, G * b + g + 1)
                nc.scalar.activation(tiles(x4_t, g), ps_z[g][:], ACT.Copy).then_inc(s_xtc, 1)
            for g in range(G):
                act.wait_ge(s_ht, G * b + g + 1)
                if g == 0 and more:
                    act.wait_ge(s_deg, DEG_UNITS * (b + 2))
                elif g == 0:
                    act.wait_ge(s_out, 16 * G * Q * b)
                nc.scalar.activation(natural(ht_hi[:], g), by_quadrant(bank(g)), ACT.Identity,
                                     bias=wb_col[:, 0:1]).then_inc(s_hthi, 1)
            for g in range(G):
                act.wait_ge(s_ut, G * b + g + 1)
                nc.scalar.activation(tiles(ut_hi, g), ps_z[g][:], ACT.Identity,
                                     bias=wb_col[:, 1:2]).then_inc(s_uthi, 1)
            for t in range(T):
                act.wait_ge(s_neg, T * b + t + 1)
                nc.scalar.activation(prob[t % RINGC][:], prob[t % RINGC][:], ACT.Exp, bias=neg_top[t % 2][:],
                                     accum_out=total[t % 2][:]).then_inc(s_exp, 1)
                if t == 0:
                    act.wait_ge(s_hspill, 16 * b + 16)
                    for s in range(2):
                        act.dma_start(h_in[s][:], h_dram[:, s * P:(s + 1) * P]).then_inc(s_hin[s], 16)
                act.wait_ge(s_hin[t % 2], 16 * (T // 2) * b + 16 * (t // 2 + 1))
                act.wait_ge(s_inv, T * b + t + 1)
                if t >= 2:
                    act.wait_ge(s_pv, T * b + t - 1)
                nc.scalar.activation(h_norm[t % 2][:], h_in[t % 2][:], ACT.Copy,
                                     scale=inv_total[t % 2][:]).then_inc(s_hnorm, 1)
                if t + 2 < T:
                    act.wait_ge(s_hnorm, T * b + t + 1)
                    act.dma_start(h_in[t % 2][:], h_dram[:, (t + 2) * P:(t + 3) * P]).then_inc(s_hin[t % 2], 16)
                if more and t == 8:
                    degree_root(act, b + 1)
            act.wait_ge(s_pv, T * b + T)
            for g in range(G):
                nc.scalar.activation(tile_major(tiles(gathered, g)), by_tile(ps_z[g][:]), ACT.Relu).then_inc(s_rel, 1)
            act.wait_ge(s_diff, G * b + G)

        def turn(dve, k, v):
            J, r = v // (N // ROWS), v % (N // ROWS)
            slot = v % NSTG
            dve.wait_ge(s_stage[slot], 16 * Q * (STAGES[slot] * k + stage_count(v, slot)))
            dst = adj_t[:, J * TG:(J + 1) * TG, r * ROWS:(r + 1) * ROWS].rearrange("p t (n r) -> p t n r", r=C)
            src = stage[slot][:].rearrange("p n (t c) -> p t n c", t=TG)
            nc.vector.transpose(dst, src).then_inc(s_turned, 1)

        def degrees(dve, k):
            dve.wait_ge(s_deg, DEG_UNITS * (k + 1))
            nc.vector.scalar_tensor_tensor(out=deg[:], in0=deg_part[:, :, 0], scalar=EPS, in1=deg_part[:, :, 1],
                                           op0=ALU.add, op1=ALU.add).then_inc(s_dsum, 1)

        def inverse_root(dve, k):
            dve.wait_ge(s_root, k + 1)
            nc.vector.reciprocal(root[:], root[:]).then_inc(s_newton, 1)
            dve.wait_ge(s_newton, 4 * k + 1)
            nc.vector.tensor_tensor(newton[:], root[:], root[:], ALU.mult).then_inc(s_newton, 1)
            dve.wait_ge(s_newton, 4 * k + 2)
            nc.vector.tensor_tensor(newton[:], newton[:], deg[:], ALU.mult).then_inc(s_newton, 1)
            dve.wait_ge(s_newton, 4 * k + 3)
            nc.vector.tensor_scalar(newton[:], newton[:], -0.5, 1.5, ALU.mult, ALU.add).then_inc(s_newton, 1)
            dve.wait_ge(s_newton, 4 * k + 4)
            nc.vector.tensor_tensor(dinv[:], newton[:], root[:], ALU.mult).then_inc(s_dinv, 1)

        def split_x_lo(dve, b, layer, g):
            dve.wait_ge(s_xhi, 12 * b + layer * G + g + 1)
            for t in range(g * TG, (g + 1) * TG):
                last = nc.vector.scalar_tensor_tensor(out=xs_lo[:, t], in0=feat[:, t], scalar=dinv[:, t:t + 1],
                                                      in1=xs_hi[:, t].bitcast(F32), op0=ALU.mult,
                                                      op1=ALU.subtract)
            last.then_inc(s_xlo, 1)

        def make_lo(eng, ops, b, u, signal):
            layer, t, h = UNITS[u]
            eng.wait_ge(s_hi, NU * b + u + 1)
            ops.tensor_tensor(a_lo[u % RINGU][:], half_columns(t, h), a_hi[u % RINGU][:].bitcast(F32),
                              ALU.subtract).then_inc(signal, 1)

        def epilogue(dve, b, layer, g):
            i = 12 * b + layer * G + g
            dve.wait_ge(s_zw, i + 1)
            for s in range(TG):
                t = g * TG + s
                yp = bank(g)[:, s * P:(s + 1) * P]
                last = nc.vector.scalar_tensor_tensor(out=yp, in0=yp, scalar=dinv[:, t:t + 1],
                                                      in1=bias[:, layer], op0=ALU.mult, op1=ALU.add)
            last.then_inc(s_affine, 1)
            dve.wait_ge(s_affine, i + 1)
            if layer < L - 1:
                nc.vector.scalar_tensor_tensor(out=tiles(feat, g), in0=bank(g), scalar=0.0, in1=tiles(feat, g),
                                               op0=ALU.max, op1=ALU.add).then_inc(s_h, 1)
            else:
                nc.vector.tensor_tensor(tiles(feat, g), bank(g), tiles(feat, g), ALU.add).then_inc(s_h, 1)

        def vector_graph(dve, b, more):
            for g in range(G):
                split_x_lo(dve, b, 0, g)
            for u in range(NU):
                if not ON_POOL[u]:
                    make_lo(dve, nc.vector, b, u, s_lo_dve)
                layer = UNITS[u][0]
                if u % (NU // L) == NU // L - 1:
                    for g in range(G):
                        epilogue(dve, b, layer, g)
                    if layer < L - 1:
                        for g in range(G):
                            split_x_lo(dve, b, layer + 1, g)
            for g in range(G):
                dve.wait_ge(s_hthi, G * b + g + 1)
                nc.vector.scalar_tensor_tensor(
                    out=natural(ht_lo[:], g), in0=by_quadrant(bank(g)), scalar=wb_col[:, 0:1],
                    in1=natural(ht_hi[:], g).bitcast(F32),
                    op0=ALU.add, op1=ALU.subtract).then_inc(s_htlo, 1)
            for g in range(G):
                dve.wait_ge(s_uthi, G * b + g + 1)
                dve.wait_ge(s_spill[g], 16 * b + 16)
                nc.vector.scalar_tensor_tensor(out=tiles(ut_lo, g), in0=ps_z[g][:], scalar=wb_col[:, 1:2],
                                               in1=tiles(ut_hi, g).bitcast(F32), op0=ALU.add,
                                               op1=ALU.subtract).then_inc(s_utlo, 1)
            for g in range(G):
                dve.wait_ge(s_hr, G * b + g + 1)
                for s in range(TG):
                    last = nc.vector.tensor_tensor(h_rows[:, g * TG + s], bank(g)[:, s * P:(s + 1) * P],
                                                   bias[:, L], ALU.add)
                last.then_inc(s_hrc, 1)
            dve.wait_ge(s_cx, b + 1)
            nc.vector.tensor_copy(coef_x[:], ps_z[0][:, 0:T]).then_inc(s_cxc, 1)
            if more:
                degrees(dve, b + 1)

            for t in range(T):
                r = prob[t % RINGC]
                if t == 1:
                    dve.wait_ge(s_hspill, 16 * b + 16)
                if t >= RINGC:
                    dve.wait_ge(s_pv, T * b + t - RINGC + 1)
                if t >= 2:
                    dve.wait_ge(s_exp, T * b + t - 1)
                for h in range(2):
                    cols = slice(h * HALF, (h + 1) * HALF)
                    if h == 1 or t > 0:
                        dve.wait_ge(s_top, 2 * T * b + 2 * t + h)
                    nc.vector.tensor_scalar(mask[:], adj_t[:, t, cols], 0.0, NEG, ALU.is_le,
                                            ALU.mult).then_inc(s_mask, 1)
                    dve.wait_ge(s_mask, 2 * T * b + 2 * t + h + 1)
                    dve.wait_ge(s_e, 2 * T * b + 2 * t + h + 1)
                    settle(dve, s_met_dve)
                    nc.vector.tensor_tensor_reduce(
                        out=r[:, cols], in0=ps_e[:, cols], in1=mask[:], scale=1.0,
                        scalar=LOWEST if h == 0 else top_half[t % 2][:], op0=ALU.add, op1=ALU.max,
                        accum_out=(top_half if h == 0 else top_full)[t % 2][:]).then_inc(s_top, 1)
                dve.wait_ge(s_top, 2 * T * b + 2 * t + 2)
                nc.vector.tensor_scalar(neg_top[t % 2][:], top_full[t % 2][:], -1.0, None,
                                        ALU.mult).then_inc(s_neg, 1)
                if more and t >= TG:
                    for v in (2 * (t - TG), 2 * (t - TG) + 1):
                        if v % 8 == 0:
                            dve.wait_ge(s_prob, T * b + TG * (v // 8) + TG)
                        turn(dve, b + 1, v)
                if more and t == 9:
                    inverse_root(dve, b + 1)
                dve.wait_ge(s_exp, T * b + t + 1)
                if t >= 2:
                    dve.wait_ge(s_hnorm, T * b + t - 1)
                nc.vector.reciprocal(inv_total[t % 2][:], total[t % 2][:]).then_inc(s_inv, 1)
            if more:
                dve.wait_ge(s_prob, T * b + T)
                for v in range(24, NV):
                    turn(dve, b + 1, v)
            dve.wait_ge(s_cg, b + 1)
            nc.vector.scalar_tensor_tensor(out=coef[:], in0=bank(3)[:, 0:T], scalar=gb[:], in1=coef_x[:],
                                           op0=ALU.add, op1=ALU.add).then_inc(s_coef, 1)
            dve.wait_ge(s_coef, b + 1)
            for g in range(G):
                dve.wait_ge(s_gt, G * b + g + 1)
                dve.wait_ge(s_back[g % 2], 32 * b + 16 * (g // 2 + 1))
                back = x4_back[g % 2]
                nc.vector.tensor_tensor(back[:], back[:], bank(g), ALU.subtract).then_inc(s_coef0, 1)
                dve.wait_ge(s_coef0, G * b + g + 1)
                for s in range(TG):
                    t = g * TG + s
                    last = nc.vector.scalar_tensor_tensor(out=gathered[:, t], in0=back[:, s * P:(s + 1) * P],
                                                          scalar=coef[:, t:t + 1],
                                                          in1=bank(g)[:, s * P:(s + 1) * P],
                                                          op0=ALU.mult, op1=ALU.add)
                last.then_inc(s_diff, 1)
                dve.wait_ge(s_diff, G * b + g + 1)
                dve.sem_inc(s_res, 1)

        def gather_unit(pe, b, u):
            layer, t, h = UNITS[u]
            if t == 0 and h == 0:
                pe.wait_ge(s_xlo, 12 * b + layer * G + 1)
            elif t % TG == 0 and h == 0:
                pe.wait_ge(s_xlo, 12 * b + layer * G + t // TG + 1)
            if t == 0 and layer > 0:
                pe.wait_ge(s_zsb, 12 * b + (layer - 1) * G + 2 * h + 2)
            signal = s_lo_pool if ON_POOL[u] else s_lo_dve
            per = POOL_PER_GRAPH if ON_POOL[u] else DVE_PER_GRAPH
            pe.wait_ge(signal, per * b + lo_count(u, ON_POOL[u]))
            hi, lo = a_hi[u % RINGU], a_lo[u % RINGU]
            g0 = 2 * h
            for g in (g0, g0 + 1):
                nc.tensor.matmul(ps_z[g][:], xs_lo[:, t], chunk_of_unit(hi, g), start=t == 0, stop=False)
            for g in (g0, g0 + 1):
                nc.tensor.matmul(ps_z[g][:], xs_hi[:, t], chunk_of_unit(hi, g), start=False, stop=False)
            for g in (g0, g0 + 1):
                last = nc.tensor.matmul(ps_z[g][:], xs_hi[:, t], chunk_of_unit(lo, g), start=False,
                                        stop=t == T - 1)
            last.then_inc(s_unit, 1)

        def weight_z(pe, b, layer, g):
            pe.wait_ge(s_zsb, 12 * b + layer * G + g + 1)
            if layer > 0:
                pe.wait_ge(s_h, 12 * b + (layer - 1) * G + g + 1)
            for s in range(TG):
                last = nc.tensor.matmul(bank(g)[:, s * P:(s + 1) * P], z_sb[g % 2][:, s * P:(s + 1) * P],
                                        w_sb[:, layer], start=True, stop=True)
            last.then_inc(s_zw, 1)

        def tensor_graph(pe, b, more):
            for u in range(NU):
                gather_unit(pe, b, u)
                layer = UNITS[u][0]
                if u % (NU // L) == NU // L - 1:
                    for g in range(G):
                        weight_z(pe, b, layer, g)
            for g in range(G):
                pe.wait_ge(s_h, 12 * b + 2 * G + g + 1)
                for s in range(TG):
                    last = nc.tensor.transpose(ps_z[g][:, s * P:(s + 1) * P], feat[:, g * TG + s], ident[:])
                last.then_inc(s_xt, 1)
            for g in range(G):
                pe.wait_ge(s_xtc, G * b + g + 1)
                nc.tensor.matmul(bank(g), ww_t[:], tile_major(tiles(x4_t, g)), start=True, stop=True).then_inc(s_ht, 1)
            for g in range(G):
                nc.tensor.matmul(ps_z[g][:], sw_t[:], tiles(x4_t, g), start=True, stop=True).then_inc(s_ut, 1)
            for g in range(G):
                pe.wait_ge(s_htlo, G * b + g + 1)
                for s in range(TG):
                    last = nc.tensor.matmul(bank(g)[:, s * P:(s + 1) * P], x4_t[:, g * TG + s], ww_t[:],
                                            start=True, stop=True)
                last.then_inc(s_hr, 1)
            pe.wait_ge(s_utlo, G * b + 1)
            for t in range(T):
                last = nc.tensor.matmul(ps_z[0][:, t:t + 1], x4_t[:, t], gate[:, 0:1], start=True, stop=True)
            last.then_inc(s_cx, 1)

            def scores(t):
                if t % TG == 0:
                    pe.wait_ge(s_utlo, G * b + t // TG + 1)
                if t == 0:
                    pe.wait_ge(s_hrc, G * b + G)
                for h in range(2):
                    if t > 0:
                        pe.wait_ge(s_top, 2 * T * b + 2 * t - 1 + h)
                    banks = (2 * h, 2 * h + 1)
                    for g in banks:
                        nc.tensor.matmul(bank(g), ut_lo[:, t], ht_hi[:, g * CH:(g + 1) * CH], start=True, stop=False)
                    for g in banks:
                        nc.tensor.matmul(bank(g), ut_hi[:, t], ht_hi[:, g * CH:(g + 1) * CH], start=False, stop=False)
                    for g in banks:
                        last = nc.tensor.matmul(bank(g), ut_hi[:, t], ht_lo[:, g * CH:(g + 1) * CH],
                                                start=False, stop=True)
                    last.then_inc(s_e, 1)

            def gather(t):
                if t == 0:
                    pe.wait_ge(s_cxc, b + 1)
                    pe.wait_ge(s_utlo, G * b + G)
                pe.wait_ge(s_prob, T * b + t + 1)
                pe.wait_ge(s_hnorm, T * b + t + 1)
                for g in range(G):
                    last = nc.tensor.matmul(ps_z[g][:], h_norm[t % 2][:], natural(prob[t % RINGC][:], g),
                                            start=t == 0, stop=t == T - 1)
                last.then_inc(s_pv, 1)

            scores(0)
            scores(1)
            for t in range(T):
                if t + 2 < T:
                    scores(t + 2)
                gather(t)
            pe.wait_ge(s_rel, G * b + G)
            pe.wait_ge(s_top, 2 * T * b + 2 * T)
            for t in range(T):
                last = nc.tensor.matmul(bank(3)[:, t:t + 1], gathered[:, t], gate[:, 1:2], start=True, stop=True)
            last.then_inc(s_cg, 1)
            for g in range(G):
                if g == 3:
                    pe.wait_ge(s_coef, b + 1)
                for s in range(TG):
                    last = nc.tensor.transpose(bank(g)[:, s * P:(s + 1) * P], gathered[:, g * TG + s], ident[:])
                last.then_inc(s_gt, 1)
            pe.wait_ge(s_diff, G * b + G)

        def pool_graph(pool, b, more):
            for u in range(NU):
                if ON_POOL[u]:
                    make_lo(pool, nc.gpsimd, b, u, s_lo_pool)
            for t in range(T):
                pool.wait_ge(s_exp, T * b + t + 1)
                r = prob[t % RINGC]
                nc.gpsimd.tensor_tensor(r[:], r[:], adj_t[:, t], ALU.mult).then_inc(s_prob, 1)

        def graphs(eng, body):
            with eng.Fori(0, B - 1) as b:
                body(eng, b, True)
            body(eng, B - 1, False)

        block = ctx.enter_context(nc.Block())

        @block.sync
        def _(sp):
            sp.dma_start(raw_ww[:], W_w).then_inc(s_const, 16)
            sp.dma_start(raw_a[:], A).then_inc(s_const, 16)
            for i, w in enumerate((W1, W2, W3)):
                sp.dma_start(w_sb[:, i], w).then_inc(s_const, 16)
            for i, row in enumerate(bias_in):
                sp.dma_start(bias[:, i], row.partition_broadcast(P)).then_inc(s_const, 16)
            sp.dma_start(wb_col[:, 0:1], W_b.rearrange("(p o) -> p o", o=1)).then_inc(s_const, 16)
            for i in range(2):
                sp.dma_start(gate[:, i:i + 1], gate_w[i * P:(i + 1) * P]).then_inc(s_const, 16)
            sp.dma_start(gb[:], gate_b.partition_broadcast(P)).then_inc(s_const, 16)
            load_x(sp, 0)
            for v in range(NSTG):
                load_stage(sp, 0, 0, v, first=True)
            load_rows(sp, 0, 0, first=True)
            for v in range(NSTG, NV):
                load_stage(sp, 0, 0, v, first=True)
            graphs(sp, sync_graph)

        @block.scalar
        def _(act):
            for d in range(DEG_UNITS):
                sum_rows(act, 0, d)
            degree_root(act, 0)
            graphs(act, scalar_graph)

        @block.gpsimd
        def _(pool):
            nc.gpsimd.memset(ident[:], 0.0).then_inc(s_ident0, 1)
            pool.wait_ge(s_ident0, 1)
            nc.gpsimd.affine_select(out=ident[:], in_=ident[:], compare_op=ALU.not_equal, fill=1.0, base=0,
                                    pattern=[[-1, P]], channel_multiplier=1).then_inc(s_ident, 1)
            graphs(pool, pool_graph)

        @block.vector
        def _(dve):
            dve.wait_ge(s_wt, 1)
            nc.vector.tensor_copy(ww_t[:], bank(0)[:, 0:P]).then_inc(s_wc, 1)
            nc.vector.tensor_tensor(a_sym[:], bank(0)[:, P:2 * P], raw_a[:], ALU.add).then_inc(s_sym, 1)
            dve.wait_ge(s_sw, 1)
            nc.vector.tensor_copy(sw_t[:], bank(1)[:, 0:P]).then_inc(s_swc, 1)
            nc.vector.tensor_copy(wb_col[:, 1:2], bank(1)[:, P:P + 1]).then_inc(s_swc, 1)
            for v in range(NV):
                turn(dve, 0, v)
            degrees(dve, 0)
            inverse_root(dve, 0)
            graphs(dve, vector_graph)

        @block.tensor
        def _(pe):
            pe.wait_ge(s_const, 16 * N_CONST)
            pe.wait_ge(s_ident, 1)
            nc.tensor.transpose(bank(0)[:, 0:P], raw_ww[:], ident[:])
            nc.tensor.transpose(bank(0)[:, P:2 * P], raw_a[:], ident[:]).then_inc(s_wt, 1)
            pe.wait_ge(s_sym, 1)
            nc.tensor.matmul(bank(1)[:, 0:P], raw_ww[:], a_sym[:], start=True, stop=True)
            nc.tensor.matmul(bank(1)[:, P:P + 1], a_sym[:], wb_col[:, 0:1], start=True,
                             stop=True).then_inc(s_sw, 1)
            pe.wait_ge(s_swc, 2)
            graphs(pe, tensor_graph)


_INS = ["x", "adj", "L0_gnn_W1", "L0_gnn_b1", "L0_gnn_W2", "L0_gnn_b2", "L0_gnn_W3", "L0_gnn_b3",
        "L1_gnn_W_w", "L1_gnn_W_b", "L1_gnn_A", "L1_gnn_gate_w", "L1_gnn_gate_b"]


def kernel(**inputs):
    import numpy as _np
    import concourse.bacc as _bacc
    from concourse import mybir as _mybir
    from concourse.bass_utils import run_bass_kernel_spmd as _run

    nc = _bacc.Bacc("TRN2", target_bir_lowering=False, num_devices=1)
    arrays, args = {}, []
    for name in _INS:
        a = _np.ascontiguousarray(inputs[name])
        arrays[f"in_{name}_dram"] = a
        args.append(nc.dram_tensor(f"in_{name}_dram", a.shape, _mybir.dt.from_np(a.dtype), kind="ExternalInput").ap())
    shape = inputs["x"].shape
    args.append(nc.dram_tensor("out_0_dram", shape, _mybir.dt.float32, kind="ExternalOutput").ap())
    gnn_kernel(nc, *args)
    r = _run(nc, [arrays], core_ids=[0])
    return r.results[0]["out_0_dram"]
```

```python
from contextlib import ExitStack

import concourse.bass as bass
from concourse import mybir

ALU = mybir.AluOpType
ACT = mybir.ActivationFunctionType
F32 = mybir.dt.float32
F32R = mybir.dt.float32r
BF16 = mybir.dt.bfloat16
AX_X = mybir.AxisListType.X

P = 128
N = 2048
Q = 4
C = 32
T = N // P
G = 4
TG = T // G
CH = N // G
L = 3
EPS = 1e-6
NEG = -9000000000000000.0
LOWEST = -3.4e38
END_AT = (17, 19, 21, 23, 25, 27)
ROWS_AT = (12, 13, 15, 16, 19, 21)
W1G = P + 1
GROUPS = [(t, min(t + 3, T)) for t in range(0, T, 3)]
NG = len(GROUPS)
OUT_PARTS = ((0, 3), (3, NG))

NU = L * T * 2
HALF = N // 2
ROWS = 256
NB = ROWS // C
NV = (N // ROWS) * G
PER_J = N // ROWS
NSTG = 3
RINGC = 3
DEG_PARTS = 4
PART = N // DEG_PARTS
DEG_UNITS = DEG_PARTS * T
SHARED = (0, 1, 2, 3, T - 2, T - 1)


def unit_order():
    order = []
    for layer in range(L):
        order += [(layer, t, h) for t in range(T - 2) for h in range(2)]
        order += [(layer, t, h) for h in range(2) for t in (T - 2, T - 1)]
    return order


UNITS = unit_order()
UL = NU // L
RING3 = 19
BUFFER = [(1, 2, 0)[u % 3] if u < RING3 else (1, 2, 0, 3)[u % 4] for u in range(NU)]


POOL_Q = [Q // 2 if u < RING3 else Q * (u % 2) if u < UL else Q * (u % UL < 4 or u % 12 in (1, 3, 6, 8, 11))
          for u in range(NU)]
ON_POOL = [q > 0 for q in POOL_Q]
ON_DVE = [q < Q for q in POOL_Q]
HI_ON_DVE = [POOL_Q[u] == Q and u >= UL and u % UL >= 4 for u in range(NU)]
POOL_PER_GRAPH = sum(ON_POOL)
DVE_PER_GRAPH = sum(ON_DVE)
HI_DVE_PER_GRAPH = sum(HI_ON_DVE)
HI_ACT_PER_GRAPH = NU - HI_DVE_PER_GRAPH

BIAS_AT = (2 * UL + 8, 2 * UL + 14, 2 * UL + 20, 2 * UL + 24)
SUM_AT = [u for u in range(UL, NU) if 2 <= u % UL < UL - 4]
SUMMED_BY = {u: DEG_UNITS * (i + 1) // len(SUM_AT) for i, u in enumerate(SUM_AT)}

NEWTON_AT = 5
NEWTON = 5
TURN_AT = (3, 5, 7, 9, 11, 13, 15, 17)
TURNS = {t: (2 * (t - TG), 2 * (t - TG) + 1) for t in range(TG, T - 2)}
TURNS[T - 1] = tuple(range(2 * (T - 2 - TG), NV - len(TURN_AT)))
TURNS_LATE = TURNS[T - 1][2:]
X_AFTER = 23

def before(u):
    return max((v for v in range(u) if BUFFER[v] == BUFFER[u]), default=None)


def count(u, chosen):
    return sum(1 for v in range(u + 1) if chosen[v])


def last_unit(layer, t):
    return max(u for u, (l, s, _) in enumerate(UNITS) if l == layer and s == t)


def chunk_done(layer, g):
    return max(u for u, (l, _, h) in enumerate(UNITS) if l == layer and h == g // 2)


def stage_count(v, slot):
    return sum(1 for w in range(v + 1) if w % NSTG == slot)


STAGES = [stage_count(NV - 1, s) for s in range(NSTG)]


def gnn_kernel(nc, x, adj, W1, b1, W2, b2, W3, b3, W_w, W_b, A, gate_w, gate_b, out):
    B = x.shape[0]
    nc.disable_value_cache = True

    with ExitStack() as ctx:
        def sem(name):
            return ctx.enter_context(nc.semaphore(name))

        base = (nc.sbuf_base + 63) // 64 * 64
        top = [base]

        def place(nbytes):
            at = top[0]
            top[0] += (nbytes + 31) // 32 * 32
            assert top[0] <= nc.sbuf_usable_end
            return at

        def sb(name, shape, dt, offset):
            return nc.alloc_sbuf_tensor_at(name, shape, dt, offset=offset)

        adj_t = sb("adj_t", [P, T, N], F32, place(T * N * 4))
        blk = [place(N * 4) for _ in range(4)]
        ring0 = place(RINGC * N * 4)
        feat = sb("feat", [P, T, P], F32, blk[0])
        deg_rows = sb("deg_rows", [P, DEG_PARTS, PART], F32, blk[1])
        xs_hi = sb("xs_hi", [P, T, P], F32R, blk[2])
        xs_lo = sb("xs_lo", [P, T, P], F32R, blk[3])
        ut_lo = sb("ut_lo", [P, T, P], F32R, blk[0])
        ht_hi = sb("ht_hi", [P, N], F32R, blk[1])
        ht_lo = sb("ht_lo", [P, N], F32R, blk[2])
        ut_hi = sb("ut_hi", [P, T, P], F32R, blk[3])
        gathered = sb("gathered", [P, T, P], F32, blk[1])
        prob = [sb(f"prob{s}", [P, N], F32, ring0 + s * N * 4) for s in range(RINGC)]
        x4_t = sb("x4_t", [P, T, P], F32, ring0 + 1 * N * 4)
        h_rows = sb("h_rows", [P, T, P], F32, ring0 + 2 * N * 4)
        stage0 = place(NSTG * NB * P * 4)
        stage = [sb(f"stage{s}", [P, NB, P], F32, stage0 + s * NB * P * 4) for s in range(NSTG)]
        pieces = [ring0 + s * N * 4 for s in range(RINGC)] + [stage0]
        a_hi = [sb(f"a_hi{s}", [P, Q, 2 * P], F32R, at) for s, at in enumerate(pieces)]
        a_lo = [sb(f"a_lo{s}", [P, Q, 2 * P], F32R, at + HALF * 4) for s, at in enumerate(pieces)]
        pair0, pair1 = place(CH * 4), place(CH * 4)
        z_sb = [sb("z_sb0", [P, CH], F32, pair0), sb("z_sb1", [P, CH], F32, pair1)]
        x4_back = [sb("x4_back0", [P, CH], F32, pair0), sb("x4_back1", [P, CH], F32, pair1)]
        mask = [sb("mask0", [P, HALF], BF16, pair0), sb("mask1", [P, HALF], BF16, pair1)]
        h_in = [sb(f"h_in{s}", [P, P], F32, place(P * 4)) for s in range(2)]
        ones = sb("ones", [P, P], F32, top[0] - 2 * P * 4)
        diag = sb("diag", [P, Q, C], F32, top[0] - P * 4)
        h_norm = [sb(f"h_norm{s}", [P, P], F32, place(P * 4)) for s in range(2)]
        w_sb = sb("w_sb", [P, L, P], F32, place(L * P * 4))
        ww_g = sb("ww_g", [P, W1G], F32, place(W1G * 4))
        sw_t = sb("sw_t", [P, P], F32, place(P * 4))
        ident_g = sb("ident_g", [P, W1G], F32, place(W1G * 4))
        ident, ww_t = ident_g[:, 0:P], ww_g[:, 0:P]
        bias = sb("bias", [P, L + 1, P], F32, place((L + 1) * P * 4))
        columns = sb("columns", [P, 14 + 10 * T], F32, place((14 + 10 * T) * 4))
        taken = [0]

        def cols(n):
            taken[0] += n
            return columns[:, taken[0] - n:taken[0]]

        wb_col = cols(2)
        gb = cols(1)
        deg_part = cols(DEG_PARTS * T).rearrange("p (t h) -> p t h", h=DEG_PARTS)
        deg, root, newton, dinv = cols(T), cols(T), cols(T), cols(T)
        top_half, top_full, neg_top, total, inv_total = ([cols(1), cols(1)] for _ in range(5))
        coef_x, coef = cols(T), cols(T)
        warm = cols(1)
        raw_ww = sb("raw_ww", [P, P], F32, ring0)
        raw_a = sb("raw_a", [P, P], F32, ring0 + P * 4)
        a_sym = sb("a_sym", [P, P], F32, ring0 + 2 * P * 4)

        ps_all = ctx.enter_context(nc.psum_tensor("ps_z", [P, N], F32))
        ps_z = [ps_all[:, g * CH:(g + 1) * CH] for g in range(G)]
        ps_e = ctx.enter_context(nc.psum_tensor("ps_e", [P, N], F32))

        def bank(g):
            return ps_e[:, g * CH:(g + 1) * CH]

        x4_dram = nc.dram_tensor("x4_dram", (P, N), F32, kind="Internal").ap()
        h_dram = nc.dram_tensor("h_dram", (P, N), F32, kind="Internal").ap()

        s_const = sem("s_const")
        s_ident0, s_ident = sem("s_ident0"), sem("s_ident")
        s_wt, s_sym, s_wc, s_sw, s_swc = sem("s_wt"), sem("s_sym"), sem("s_wc"), sem("s_sw"), sem("s_swc")
        s_x = [sem(f"s_x{i}") for i in range(2)]
        s_rows = [sem(f"s_rows{s}") for s in range(DEG_PARTS)]
        s_deg = sem("s_deg")
        s_degadd = sem("s_degadd")
        s_dsum, s_root, s_newton, s_dinv = sem("s_dsum"), sem("s_root"), sem("s_newton"), sem("s_dinv")
        s_stage = [sem(f"s_stage{s}") for s in range(NSTG)]
        s_turned = sem("s_turned")
        s_hi_act, s_hi_dve = sem("s_hi_act"), sem("s_hi_dve")
        s_lo_dve, s_lo_pool = sem("s_lo_dve"), sem("s_lo_pool")
        s_unit = sem("s_unit")
        s_zsb, s_zw, s_affine, s_h = sem("s_zsb"), sem("s_zw"), sem("s_affine"), sem("s_h")
        s_hb = sem("s_hb")
        s_xhi, s_xlo = sem("s_xhi"), sem("s_xlo")
        s_spill = [sem(f"s_spill{g}") for g in range(G)]
        s_xt, s_xtc = sem("s_xt"), sem("s_xtc")
        s_ht, s_hthi, s_htlo = sem("s_ht"), sem("s_hthi"), sem("s_htlo")
        s_ut, s_uthi, s_utlo = sem("s_ut"), sem("s_uthi"), sem("s_utlo")
        s_hr, s_hrc, s_hrb = sem("s_hr"), sem("s_hrc"), sem("s_hrb")
        s_hspill = [sem(f"s_hspill{i}") for i in range(NG)]
        s_e = sem("s_e")
        s_mask, s_top, s_neg = sem("s_mask"), sem("s_top"), sem("s_neg")
        s_exp, s_prob, s_prob_dve = sem("s_exp"), sem("s_prob"), sem("s_prob_dve")
        s_inv, s_hnorm = sem("s_inv"), sem("s_hnorm")
        s_hin = [sem(f"s_hin{s}") for s in range(2)]
        s_pv = sem("s_pv")
        s_rel_act, s_rel_dve = sem("s_rel_act"), sem("s_rel_dve")
        s_coef, s_gt, s_minus = sem("s_coef"), sem("s_gt"), sem("s_minus")
        s_back = [sem(f"s_back{s}") for s in range(2)]
        s_diff = sem("s_diff")
        s_out = sem("s_out")
        s_ones, s_degp, s_newton0 = sem("s_ones"), sem("s_degp"), sem("s_newton0")

        s_met_dve, s_met_sp = sem("s_met_dve"), sem("s_met_sp")

        def natural(ap, g):
            return ap.rearrange("p (q g x) -> p g q x", q=Q, g=G)[:, g]

        def chunk_of_unit(buf, g):
            return buf[:, :, (g % 2) * P:(g % 2 + 1) * P]

        def half_columns(t, h):
            return adj_t[:, t].rearrange("p (q h x) -> p h q x", q=Q, h=2)[:, h]

        def by_tile(ap):
            return ap.rearrange("p (q s c) -> p q s c", q=Q, s=TG)

        def tile_major(ap):
            return ap.rearrange("p (s q c) -> p q s c", q=Q, s=TG)

        def by_quadrant(ap):
            return ap.rearrange("p (q x) -> p q x", q=Q)

        def tiles(buf, g):
            return buf[:, g * TG:(g + 1) * TG].rearrange("p s f -> p (s f)")

        def node_rows(dram, quadrant, t0, t1):
            per = N // Q
            return dram[quadrant * per + t0 * C:quadrant * per + t1 * C].rearrange("(t c) f -> c t f", c=C)

        def group(bank_ap, n):
            wide = bank_ap[:, 0:n * W1G].rearrange("p (s f) -> p s f", f=W1G)
            return wide[:, :, 0:P], bank_ap[:, P:n * W1G:W1G]

        bias_in = [b1, b2, b3, W_b]
        N_CONST = 5 + len(bias_in) + 4

        def settle(eng, passed):
            eng.sem_inc(passed, 1)

        OUT_INC = 16 * Q * len(OUT_PARTS)

        def load_x(sp, b, half):
            t0, t1 = half * T // 2, (half + 1) * T // 2
            for q in range(Q):
                sp.dma_start(feat[q * C:(q + 1) * C, t0:t1], node_rows(x[b], q, t0, t1)).then_inc(s_x[half], 16)

        def load_rows(sp, b):
            for d in range(DEG_UNITS):
                t, h = d // DEG_PARTS, d % DEG_PARTS
                if t > 0:
                    sp.wait_ge(s_deg, DEG_UNITS * b + d - DEG_PARTS + 1)
                sp.dma_start(deg_rows[:, h], adj[b + 1, t * P:(t + 1) * P, h * PART:(h + 1) * PART]
                             ).then_inc(s_rows[h], 16)

        def load_stage(sp, b, k, v, first=False):
            if v >= NSTG or not first:
                sp.wait_ge(s_turned, NV * k + max(v - NSTG + 1, 0))
            J, r = v // (N // ROWS), v % (N // ROWS)
            for q in range(Q):
                col = q * (N // Q) + J * P
                src = adj[b, r * ROWS:(r + 1) * ROWS, col:col + P].rearrange("(n c) j -> c n j", c=C)
                sp.dma_start(stage[v % NSTG][q * C:(q + 1) * C], src).then_inc(s_stage[v % NSTG], 16)

        def sync_end(sp, b):
            sp.wait_ge(s_top, 2 * T * b + 2 * T)
            for i, (t0, t1) in enumerate(GROUPS):
                if i >= 2:
                    sp.wait_ge(s_diff, NG * b + i - 1)
                sp.dma_start(x4_back[i % 2][:, 0:(t1 - t0) * P], x4_dram[:, t0 * P:t1 * P]).then_inc(s_back[i % 2], 16)
            for i0, i1 in OUT_PARTS:
                sp.wait_ge(s_diff, NG * b + i1)
                t0, t1 = GROUPS[i0][0], GROUPS[i1 - 1][1]
                for q in range(Q):
                    sp.dma_start(node_rows(out[b], q, t0, t1), gathered[q * C:(q + 1) * C, t0:t1]).then_inc(s_out, 16)
            sp.wait_ge(s_out, OUT_INC * b + OUT_INC)

        def sync_layers(sp, b, end, more):
            if end:
                sync_end(sp, b - 1)
            if more:
                load_rows(sp, b)
            for g in range(G):
                sp.wait_ge(s_h, 12 * b + 2 * G + g + 1)
                sp.dma_start(x4_dram[:, g * CH:(g + 1) * CH], tiles(feat, g)).then_inc(s_spill[g], 16)
            for i, (t0, t1) in enumerate(GROUPS):
                sp.wait_ge(s_hrb, NG * b + i + 1)
                sp.dma_start(h_dram[:, t0 * P:t1 * P],
                             h_rows[:, t0:t1].rearrange("p t f -> p (t f)")).then_inc(s_hspill[i], 16)

        def sync_attention(sp, b, more):
            if more:
                for v in range(NV):
                    load_stage(sp, b + 1, b + 1, v)
                    if v == 2 * (T // 2 + 2 - TG):
                        sp.wait_ge(s_e, 2 * T * b + T)
                        load_x(sp, b + 1, 0)
                    if v == X_AFTER:
                        sp.wait_ge(s_e, 2 * T * b + 2 * T)
                        load_x(sp, b + 1, 1)
            settle(sp, s_met_sp)

        def sum_rows(act, b, d):
            t, h = d // DEG_PARTS, d % DEG_PARTS
            act.wait_ge(s_rows[h], 16 * T * b + 16 * (t + 1))
            nc.scalar.activation(deg_rows[:, h], deg_rows[:, h], ACT.Copy,
                                 accum_out=deg_part[:, t, h:h + 1]).then_inc(s_deg, 1)

        def dinv_by_node(act, k, q):
            act.wait_ge(s_newton, NEWTON * k + NEWTON)
            for s in range(TG):
                last = nc.scalar.activation(dinv[q * C:(q + 1) * C, s:T:TG],
                                            newton[s * C:(s + 1) * C, q * G:(q + 1) * G], ACT.Copy)
            if q == Q - 1:
                last.then_inc(s_dinv, 1)

        def degree_root(act, k):
            act.wait_ge(s_dsum, k + 1)
            nc.scalar.activation(root[:], deg[:], ACT.Sqrt).then_inc(s_root, 1)

        def split_x(act, b, end, layer, t):
            if layer == 0 and t % (T // 2) == 0:
                act.wait_ge(s_x[t // (T // 2)], 16 * Q * b + 16 * Q)
            if layer == 0 and t == 0:
                act.wait_ge(s_dinv, b + 1)
                if end:
                    act.wait_ge(s_e, 2 * T * b)
            elif layer > 0:
                act.wait_ge(s_h, 12 * b + (layer - 1) * G + t // TG + 1)
                act.wait_ge(s_unit, NU * b + last_unit(layer - 1, t) + 1)
            nc.scalar.activation(xs_hi[:, t], feat[:, t], ACT.Copy, scale=dinv[:, t:t + 1]).then_inc(s_xhi, 1)

        def wait_buffer(eng, b, end, u):
            layer, t, _ = UNITS[u]
            if before(u) is not None:
                eng.wait_ge(s_unit, NU * b + before(u) + 1)
            elif BUFFER[u] < RINGC and end:
                eng.wait_ge(s_pv, T * b - RINGC + 1 + u)
            if layer == 0:
                eng.wait_ge(s_turned, NV * b + (NV if BUFFER[u] == RINGC else PER_J * (t // TG) + PER_J))

        def make_hi(act, b, end, u):
            layer, t, h = UNITS[u]
            wait_buffer(act, b, end, u)
            nc.scalar.activation(a_hi[BUFFER[u]][:], half_columns(t, h), ACT.Copy).then_inc(s_hi_act, 1)

        def move_z(act, b, end, layer, g):
            i = layer * G + g
            act.wait_ge(s_unit, NU * b + chunk_done(layer, g) + 1)
            if i == 0 and end:
                act.wait_ge(s_diff, NG * b)
            if i >= 2:
                act.wait_ge(s_zw, 12 * b + i - 1)
            nc.scalar.activation(tile_major(z_sb[g % 2][:]), by_tile(ps_z[g]), ACT.Copy).then_inc(s_zsb, 1)

        def scalar_end(act, b):
            act.wait_ge(s_pv, T * b + T)
            for g in range(0, G, 2):
                nc.scalar.activation(tile_major(tiles(gathered, g)), by_tile(ps_z[g]), ACT.Relu).then_inc(s_rel_act, 1)

        def scalar_layers(act, b, end, more):
            summed = 0
            for u in range(NU):
                layer, since = UNITS[u][0], u % UL
                if layer == 0:
                    if since == 0:
                        split_x(act, b, end, 0, 0)
                    if since == 2:
                        if end:
                            scalar_end(act, b - 1)
                    if 2 <= since < T + 1:
                        split_x(act, b, end, 0, since - 1)
                else:
                    if since == 1:
                        move_z(act, b, end, layer - 1, 0)
                        move_z(act, b, end, layer - 1, 1)
                    if since == 3:
                        split_x(act, b, end, layer, 0)
                        move_z(act, b, end, layer - 1, 2)
                        move_z(act, b, end, layer - 1, 3)
                    if since == 4:
                        for t in range(1, TG):
                            split_x(act, b, end, layer, t)
                    if 0 <= since - 6 < T - TG:
                        split_x(act, b, end, layer, since - 6 + TG)
                if not HI_ON_DVE[u]:
                    make_hi(act, b, end, u)
                while more and summed < SUMMED_BY.get(u, 0):
                    sum_rows(act, b, summed)
                    summed += 1
            for g in range(G):
                move_z(act, b, end, L - 1, g)

            def transposed(g):
                act.wait_ge(s_xt, G * b + g + 1)
                nc.scalar.activation(tiles(x4_t, g), ps_z[g], ACT.Copy).then_inc(s_xtc, 1)

            def h_transposed(g):
                act.wait_ge(s_ht, G * b + g + 1)
                if g == 0 and not more:
                    act.wait_ge(s_out, OUT_INC * b)
                nc.scalar.activation(natural(ht_hi[:], g), by_quadrant(bank(g)), ACT.Identity,
                                     bias=wb_col[:, 0:1]).then_inc(s_hthi, 1)

            transposed(0)
            for g in range(G):
                if g + 1 < G:
                    transposed(g + 1)
                h_transposed(g)
                act.wait_ge(s_ut, G * b + g + 1)
                nc.scalar.activation(tiles(ut_hi, g), ps_z[g][:], ACT.Identity,
                                     bias=wb_col[:, 1:2]).then_inc(s_uthi, 1)

        def scalar_attention(act, b, more):
            def load_h(t):
                act.wait_ge(s_hspill[t // 3], 16 * b + 16)
                if t >= 3:
                    act.wait_ge(s_hnorm, T * b + t - 1)
                act.dma_start(h_in[t % 2][:], h_dram[:, t * P:(t + 1) * P]).then_inc(s_hin[t % 2], 16)

            def normalize(t):
                if t > 0:
                    act.wait_ge(s_hin[t % 2], 16 * (T // 2 - 1 + t % 2) * b + 16 * ((t + 1) // 2))
                act.wait_ge(s_inv, T * b + t + 1)
                if t == 0:
                    act.wait_ge(s_hrb, NG * b + 1)
                if t >= 2:
                    act.wait_ge(s_pv, T * b + t - 1)
                nc.scalar.activation(h_norm[t % 2][:], h_rows[:, 0] if t == 0 else h_in[t % 2][:], ACT.Copy,
                                     scale=inv_total[t % 2][:]).then_inc(s_hnorm, 1)
                if 0 < t and t + 2 < T:
                    load_h(t + 2)

            if more:
                degree_root(act, b + 1)
                nc.scalar.activation(warm[:], wb_col[:, 0:1], ACT.Exp)
            for i, (t0, t1) in enumerate(GROUPS):
                act.wait_ge(s_hr, NG * b + i + 1)
                rows, gates = group(ps_z[i % G], t1 - t0)
                nc.scalar.activation(h_rows[:, t0:t1], rows, ACT.Copy)
                nc.scalar.activation(coef_x[:, t0:t1], gates, ACT.Copy).then_inc(s_hrc, 1)
            for t in range(T):
                act.wait_ge(s_top, 2 * T * b + 2 * t + 2)
                if t >= 2:
                    act.wait_ge(s_exp, T * b + t - 1)
                nc.scalar.activation(neg_top[t % 2][:], top_full[t % 2][:], ACT.Copy,
                                     scale=-1.0).then_inc(s_neg, 1)
                act.wait_ge(s_neg, T * b + t + 1)
                if t >= 2:
                    act.wait_ge(s_inv, T * b + t - 1)
                nc.scalar.activation(prob[t % RINGC][:], prob[t % RINGC][:], ACT.Exp, bias=neg_top[t % 2][:],
                                     accum_out=total[t % 2][:]).then_inc(s_exp, 1)
                normalize(t)
                if t == 0:
                    load_h(1)
                    load_h(2)
                if more and 0 <= t - NEWTON_AT - NEWTON < Q:
                    dinv_by_node(act, b + 1, t - NEWTON_AT - NEWTON)

        def turn(dve, k, v):
            J, r = v // (N // ROWS), v % (N // ROWS)
            slot = v % NSTG
            dve.wait_ge(s_stage[slot], 16 * Q * (STAGES[slot] * k + stage_count(v, slot)))
            dst = adj_t[:, J * TG:(J + 1) * TG, r * ROWS:(r + 1) * ROWS].rearrange("p t (n r) -> p t n r", r=C)
            src = stage[slot][:].rearrange("p n (t c) -> p t n c", t=TG)
            nc.vector.transpose(dst, src).then_inc(s_turned, 1)

        def degrees(dve, b):
            dve.wait_ge(s_deg, DEG_UNITS * b + DEG_UNITS)
            nc.vector.scalar_tensor_tensor(out=deg[:], in0=deg_part[:, :, 0], scalar=EPS, in1=deg_part[:, :, 1],
                                           op0=ALU.add, op1=ALU.add).then_inc(s_degadd, 1)
            nc.vector.tensor_tensor(newton[:], deg_part[:, :, 2], deg_part[:, :, 3], ALU.add).then_inc(s_degadd, 1)
            dve.wait_ge(s_degadd, 2 * b + 2)
            nc.vector.tensor_tensor(deg[:], deg[:], newton[:], ALU.add).then_inc(s_dsum, 1)

        def first_degrees(dve):
            dve.wait_ge(s_degp, 1)
            dve.wait_ge(s_ident, 1)
            row = ps_all[:].rearrange("p (q t c) -> p t q c", q=Q, c=C)
            for t in range(T):
                if t > 0:
                    dve.wait_ge(s_newton0, t)
                nc.vector.tensor_tensor_reduce(
                    out=diag[:], in0=row[:, t], in1=ident.rearrange("p (q c) -> p q c", q=Q), scale=1.0,
                    scalar=EPS, op0=ALU.mult, op1=ALU.add, accum_out=deg[:, t:t + 1]).then_inc(s_newton0, 1)
            dve.wait_ge(s_newton0, T)
            dve.sem_inc(s_dsum, 1)

        def newton_step(dve, k, i):
            if i == 0:
                dve.wait_ge(s_root, k + 1)
                nc.vector.reciprocal(root[:], root[:]).then_inc(s_newton, 1)
                return
            dve.wait_ge(s_newton, NEWTON * k + i)
            if i == 1:
                nc.vector.tensor_tensor(newton[:], root[:], root[:], ALU.mult).then_inc(s_newton, 1)
            elif i == 2:
                nc.vector.tensor_tensor(newton[:], newton[:], deg[:], ALU.mult).then_inc(s_newton, 1)
            elif i == 3:
                nc.vector.tensor_scalar(newton[:], newton[:], -0.5, 1.5, ALU.mult, ALU.add).then_inc(s_newton, 1)
            else:
                nc.vector.tensor_tensor(newton[:], newton[:], root[:], ALU.mult).then_inc(s_newton, 1)

        def split_x_lo(dve, b, layer, t):
            dve.wait_ge(s_xhi, L * T * b + layer * T + t + 1)
            nc.vector.scalar_tensor_tensor(out=xs_lo[:, t], in0=feat[:, t], scalar=dinv[:, t:t + 1],
                                           in1=xs_hi[:, t].bitcast(F32), op0=ALU.mult,
                                           op1=ALU.subtract).then_inc(s_xlo, 1)

        def make_hi_dve(dve, b, end, u):
            _, t, h = UNITS[u]
            wait_buffer(dve, b, end, u)
            nc.vector.tensor_copy(a_hi[BUFFER[u]][:], half_columns(t, h)).then_inc(s_hi_dve, 1)

        def make_lo(eng, ops, b, u, signal):
            _, t, h = UNITS[u]
            if HI_ON_DVE[u]:
                eng.wait_ge(s_hi_dve, HI_DVE_PER_GRAPH * b + count(u, HI_ON_DVE))
            else:
                eng.wait_ge(s_hi_act, HI_ACT_PER_GRAPH * b + u + 1 - count(u, HI_ON_DVE))
            part = slice(0, POOL_Q[u]) if signal is s_lo_pool else slice(POOL_Q[u], Q)
            ops.tensor_tensor(a_lo[BUFFER[u]][:, part], half_columns(t, h)[:, part],
                              a_hi[BUFFER[u]][:, part].bitcast(F32), ALU.subtract).then_inc(signal, 1)

        def epilogue(dve, b, layer, g):
            i = 12 * b + layer * G + g
            dve.wait_ge(s_zw, i + 1)
            if layer == L - 1:
                dve.wait_ge(s_hb, G * b + g + 1)
                for s in range(TG):
                    t = g * TG + s
                    last = nc.vector.scalar_tensor_tensor(out=feat[:, t], in0=bank(g)[:, s * P:(s + 1) * P],
                                                          scalar=dinv[:, t:t + 1], in1=feat[:, t],
                                                          op0=ALU.mult, op1=ALU.add)
                last.then_inc(s_h, 1)
                return
            for s in range(TG):
                t = g * TG + s
                yp = bank(g)[:, s * P:(s + 1) * P]
                last = nc.vector.scalar_tensor_tensor(out=yp, in0=yp, scalar=dinv[:, t:t + 1],
                                                      in1=bias[:, layer], op0=ALU.mult, op1=ALU.add)
            last.then_inc(s_affine, 1)
            dve.wait_ge(s_affine, (L - 1) * G * b + layer * G + g + 1)
            nc.vector.scalar_tensor_tensor(out=tiles(feat, g), in0=bank(g), scalar=0.0, in1=tiles(feat, g),
                                           op0=ALU.max, op1=ALU.add).then_inc(s_h, 1)

        def end_group(dve, b, i):
            t0, t1 = GROUPS[i]
            n = t1 - t0
            dve.wait_ge(s_gt, NG * b + i + 1)
            rows, gates = group(bank(i % G), n)
            nc.vector.scalar_tensor_tensor(out=coef[:, t0:t1], in0=gates, scalar=gb[:], in1=coef_x[:, t0:t1],
                                           op0=ALU.add, op1=ALU.add).then_inc(s_coef, 1)
            dve.wait_ge(s_back[i % 2], 16 * (NG // 2) * b + 16 * (i // 2 + 1))
            back = x4_back[i % 2][:, 0:n * P].rearrange("p (s f) -> p s f", f=P)
            nc.vector.tensor_tensor(back, back, rows, ALU.subtract).then_inc(s_minus, 1)
            dve.wait_ge(s_coef, NG * b + i + 1)
            dve.wait_ge(s_minus, NG * b + i + 1)
            for s in range(n):
                last = nc.vector.scalar_tensor_tensor(out=gathered[:, t0 + s], in0=back[:, s],
                                                      scalar=coef[:, t0 + s:t0 + s + 1], in1=rows[:, s],
                                                      op0=ALU.mult, op1=ALU.add)
            last.then_inc(s_diff, 1)

        def relu_gathered(dve, b):
            dve.wait_ge(s_pv, T * b + T)
            for g in range(1, G, 2):
                for s in range(TG):
                    last = nc.vector.tensor_scalar(
                        gathered[:, g * TG + s].rearrange("p (q c) -> p q c", q=Q),
                        ps_z[g].rearrange("p (q s c) -> p s q c", q=Q, s=TG)[:, s], 0.0, None, ALU.max)
                last.then_inc(s_rel_dve, 1)

        def vector_end(dve, b):
            relu_gathered(dve, b)
            for i in range(NG):
                end_group(dve, b, i)

        def vector_layers(dve, b, end, more):
            for u in range(NU):
                layer, since = UNITS[u][0], u % UL
                if layer == 0:
                    if end and since in TURN_AT:
                        turn(dve, b, NV - len(TURN_AT) + TURN_AT.index(since))
                    if since == 0:
                        split_x_lo(dve, b, 0, 0)
                    if since == 1:
                        if end:
                            relu_gathered(dve, b - 1)
                    if 1 <= since < T:
                        split_x_lo(dve, b, 0, since)
                    if end and since in END_AT:
                        end_group(dve, b - 1, END_AT.index(since))
                else:
                    if since == 0:
                        epilogue(dve, b, layer - 1, 0)
                        split_x_lo(dve, b, layer, 0)
                        epilogue(dve, b, layer - 1, 1)
                        for t in range(1, TG):
                            split_x_lo(dve, b, layer, t)
                        epilogue(dve, b, layer - 1, 2)
                    if since == 5:
                        epilogue(dve, b, layer - 1, 3)
                    if 0 <= since - 6 < T - TG:
                        split_x_lo(dve, b, layer, since - 6 + TG)
                if u + 1 < NU and HI_ON_DVE[u + 1]:
                    make_hi_dve(dve, b, end, u + 1)
                if ON_DVE[u]:
                    make_lo(dve, nc.vector, b, u, s_lo_dve)
            for g in range(G):
                epilogue(dve, b, L - 1, g)
            if more:
                degrees(dve, b)
            for g in range(G):
                dve.wait_ge(s_hthi, G * b + g + 1)
                nc.vector.scalar_tensor_tensor(
                    out=natural(ht_lo[:], g), in0=by_quadrant(bank(g)), scalar=wb_col[:, 0:1],
                    in1=natural(ht_hi[:], g).bitcast(F32),
                    op0=ALU.add, op1=ALU.subtract).then_inc(s_htlo, 1)
                dve.wait_ge(s_uthi, G * b + g + 1)
                dve.wait_ge(s_spill[g], 16 * b + 16)
                nc.vector.scalar_tensor_tensor(out=tiles(ut_lo, g), in0=ps_z[g], scalar=wb_col[:, 1:2],
                                               in1=tiles(ut_hi, g).bitcast(F32), op0=ALU.add,
                                               op1=ALU.subtract).then_inc(s_utlo, 1)

        def vector_attention(dve, b, more):
            def inverse_total(t):
                dve.wait_ge(s_exp, T * b + t + 1)
                if t >= 2:
                    dve.wait_ge(s_hnorm, T * b + t - 1)
                nc.vector.reciprocal(inv_total[t % 2][:], total[t % 2][:]).then_inc(s_inv, 1)

            def make_mask(t, h):
                if t > 0:
                    dve.wait_ge(s_top, 2 * T * b + 2 * t + h - 1)
                else:
                    dve.wait_ge(s_zw, 12 * (b + 1) - 1 + h)
                nc.vector.tensor_scalar(mask[h][:], adj_t[:, t, h * HALF:(h + 1) * HALF], 0.0, NEG, ALU.is_le,
                                        ALU.mult).then_inc(s_mask, 1)

            def mask_scores(t, h):
                cols = slice(h * HALF, (h + 1) * HALF)
                dve.wait_ge(s_mask, 2 * T * b + 2 * t + h + 1)
                dve.wait_ge(s_e, 2 * T * b + 2 * t + h + 1)
                if h == 1:
                    dve.wait_ge(s_top, 2 * T * b + 2 * t + 1)
                settle(dve, s_met_dve)
                nc.vector.tensor_tensor_reduce(
                    out=prob[t % RINGC][:, cols], in0=ps_e[:, cols], in1=mask[h][:], scale=1.0,
                    scalar=LOWEST if h == 0 else top_half[t % 2][:], op0=ALU.add, op1=ALU.max,
                    accum_out=(top_half if h == 0 else top_full)[t % 2][:]).then_inc(s_top, 1)

            def end_exp(t):
                inverse_total(t)
                if t in SHARED:
                    nc.vector.tensor_tensor(prob[t % RINGC][:, HALF:], prob[t % RINGC][:, HALF:],
                                            adj_t[:, t, HALF:], ALU.mult).then_inc(s_prob_dve, 1)

            def turn_next(v):
                if v % PER_J == 0:
                    dve.wait_ge(s_prob, T * b + TG * (v // PER_J) + TG)
                turn(dve, b + 1, v)

            late = [t for t in range(T - 1) if not more or t < TG or t == T - 2]
            make_mask(0, 0)
            make_mask(0, 1)
            for t in range(T):
                if t == 2:
                    for i in range(NG):
                        dve.wait_ge(s_hspill[i], 16 * b + 16)
                    dve.wait_ge(s_hnorm, T * b + 1)
                if t == 1:
                    dve.wait_ge(s_hr, NG * b + NG)
                if t >= RINGC:
                    dve.wait_ge(s_pv, T * b + t - RINGC + 1)
                if t >= 2:
                    dve.wait_ge(s_neg, T * b + t - 1)
                mask_scores(t, 0)
                mask_scores(t, 1)
                if t - 1 in late:
                    end_exp(t - 1)
                stagings = [v for v in TURNS.get(t, ()) if v not in TURNS_LATE] if more else []
                for h in range(2):
                    if t + 1 < T:
                        make_mask(t + 1, h)
                    for v in stagings[h:h + 1]:
                        turn_next(v)
                if more and 0 <= t - NEWTON_AT < NEWTON:
                    newton_step(dve, b + 1, t - NEWTON_AT)
                if t not in late:
                    end_exp(t)
            if more:
                for v in TURNS_LATE:
                    turn_next(v)

        def gather_unit(pe, b, end, u):
            layer, t, h = UNITS[u]
            if h == 0:
                pe.wait_ge(s_xlo, L * T * b + layer * T + t + 1)
            if t == 0 and layer > 0:
                pe.wait_ge(s_zsb, 12 * b + (layer - 1) * G + 2 * h + 2)
            elif t == 0 and end:
                pe.wait_ge(s_rel_act, 2 * b - 1 + h)
                pe.wait_ge(s_rel_dve, 2 * b - 1 + h)
            if ON_POOL[u]:
                pe.wait_ge(s_lo_pool, POOL_PER_GRAPH * b + count(u, ON_POOL))
            if ON_DVE[u]:
                pe.wait_ge(s_lo_dve, DVE_PER_GRAPH * b + count(u, ON_DVE))
            hi, lo = a_hi[BUFFER[u]], a_lo[BUFFER[u]]
            pair = (2 * h, 2 * h + 1)
            for g in pair:
                nc.tensor.matmul(ps_z[g], xs_lo[:, t], chunk_of_unit(hi, g), start=t == 0, stop=False)
            for g in pair:
                nc.tensor.matmul(ps_z[g], xs_hi[:, t], chunk_of_unit(hi, g), start=False, stop=False)
            for g in pair:
                last = nc.tensor.matmul(ps_z[g], xs_hi[:, t], chunk_of_unit(lo, g), start=False,
                                        stop=t == T - 1)
            last.then_inc(s_unit, 1)

        def weight_z(pe, b, end, layer, g):
            pe.wait_ge(s_zsb, 12 * b + layer * G + g + 1)
            if layer > 0:
                pe.wait_ge(s_h, 12 * b + (layer - 1) * G + g + 1)
            elif end and g == 0:
                pe.wait_ge(s_diff, NG * b)
            for s in range(TG):
                last = nc.tensor.matmul(bank(g)[:, s * P:(s + 1) * P], z_sb[g % 2][:, s * P:(s + 1) * P],
                                        w_sb[:, layer], start=True, stop=True)
            last.then_inc(s_zw, 1)

        def rows_of_gathered(pe, b, i):
            t0, t1 = GROUPS[i]
            if i == 0:
                pe.wait_ge(s_rel_act, 2 * b + 2)
                pe.wait_ge(s_rel_dve, 2 * b + 2)
                pe.wait_ge(s_top, 2 * T * b + 2 * T)
            if i >= G:
                pe.wait_ge(s_diff, NG * b + i - G + 1)
            for s in range(t1 - t0):
                last = nc.tensor.matmul(bank(i % G)[:, s * W1G:(s + 1) * W1G], gathered[:, t0 + s], ident_g[:],
                                        start=True, stop=True)
            last.then_inc(s_gt, 1)

        def tensor_end(pe, b):
            for i in range(NG):
                rows_of_gathered(pe, b, i)

        def tensor_layers(pe, b, end, more):
            for u in range(NU):
                layer, since = UNITS[u][0], u % UL
                if since == UL - 1:
                    weight_z(pe, b, end, layer, 0)
                    weight_z(pe, b, end, layer, 1)
                gather_unit(pe, b, end, u)
                if since == UL - 1 and layer < L - 1:
                    weight_z(pe, b, end, layer, 2)
                    weight_z(pe, b, end, layer, 3)
                if end and u in ROWS_AT:
                    rows_of_gathered(pe, b - 1, ROWS_AT.index(u))

            def transpose_x(g):
                pe.wait_ge(s_h, 12 * b + 2 * G + g + 1)
                for s in range(TG):
                    last = nc.tensor.transpose(ps_z[g][:, s * P:(s + 1) * P], feat[:, g * TG + s], ident)
                last.then_inc(s_xt, 1)

            weight_z(pe, b, end, L - 1, 2)
            transpose_x(0)
            weight_z(pe, b, end, L - 1, 3)
            for g in range(G):
                if g + 1 < G:
                    transpose_x(g + 1)
                pe.wait_ge(s_xtc, G * b + g + 1)
                nc.tensor.matmul(bank(g), ww_t, tile_major(tiles(x4_t, g)), start=True, stop=True).then_inc(s_ht, 1)
                nc.tensor.matmul(ps_z[g], sw_t[:], tiles(x4_t, g), start=True, stop=True).then_inc(s_ut, 1)

        def tensor_attention(pe, b, more):
            def rows_of_h(i):
                t0, t1 = GROUPS[i]
                if i < G:
                    pe.wait_ge(s_utlo, G * b + i + 1)
                else:
                    pe.wait_ge(s_hrc, NG * b + i - G + 1)
                for s in range(t1 - t0):
                    last = nc.tensor.matmul(ps_z[i % G][:, s * W1G:(s + 1) * W1G], x4_t[:, t0 + s], ww_g[:],
                                            start=True, stop=True)
                last.then_inc(s_hr, 1)

            def scores(t):
                if t % TG == 0:
                    pe.wait_ge(s_utlo, G * b + t // TG + 1)
                if t == 0:
                    pe.wait_ge(s_htlo, G * b + G)
                for h in range(2):
                    if t > 0:
                        pe.wait_ge(s_top, 2 * T * b + 2 * t - 1 + h)
                    banks = (2 * h, 2 * h + 1)
                    for g in banks:
                        nc.tensor.matmul(bank(g), ut_lo[:, t], ht_hi[:, g * CH:(g + 1) * CH], start=True, stop=False)
                    for g in banks:
                        nc.tensor.matmul(bank(g), ut_hi[:, t], ht_hi[:, g * CH:(g + 1) * CH], start=False, stop=False)
                    for g in banks:
                        last = nc.tensor.matmul(bank(g), ut_hi[:, t], ht_lo[:, g * CH:(g + 1) * CH],
                                                start=False, stop=True)
                    last.then_inc(s_e, 1)

            def gather(t):
                if t == 0:
                    pe.wait_ge(s_hrc, NG * b + NG)
                pe.wait_ge(s_prob, T * b + t + 1)
                if t in SHARED:
                    pe.wait_ge(s_prob_dve, len(SHARED) * b + SHARED.index(t) + 1)
                pe.wait_ge(s_hnorm, T * b + t + 1)
                for g in range(G):
                    last = nc.tensor.matmul(ps_z[g], h_norm[t % 2][:], natural(prob[t % RINGC][:], g),
                                            start=t == 0, stop=t == T - 1)
                last.then_inc(s_pv, 1)

            scores(0)
            for i in range(NG):
                rows_of_h(i)
            scores(1)
            for t in range(T):
                if t + 2 < T:
                    scores(t + 2)
                gather(t)

        def pool_layers(pool, b, end, more):
            for u in range(NU):
                if ON_POOL[u]:
                    make_lo(pool, nc.gpsimd, b, u, s_lo_pool)
                if u in BIAS_AT:
                    g = BIAS_AT.index(u)
                    pool.wait_ge(s_xlo, L * T * b + (L - 1) * T + (g + 1) * TG)
                    h = feat[:, g * TG:(g + 1) * TG]
                    nc.gpsimd.tensor_tensor(h, h, bias[:, L - 1:L].broadcast_to([P, TG, P]), ALU.add).then_inc(s_hb, 1)

        def pool_attention(pool, b, more):
            for i, (t0, t1) in enumerate(GROUPS):
                pool.wait_ge(s_hrc, NG * b + i + 1)
                r = h_rows[:, t0:t1]
                nc.gpsimd.tensor_tensor(r, r, bias[:, L:L + 1].broadcast_to([P, t1 - t0, P]), ALU.add).then_inc(s_hrb, 1)
            for t in range(T):
                pool.wait_ge(s_exp, T * b + t + 1)
                cols = slice(0, HALF if t in SHARED else N)
                r = prob[t % RINGC][:, cols]
                nc.gpsimd.tensor_tensor(r, r, adj_t[:, t, cols], ALU.mult).then_inc(s_prob, 1)

        def graphs(eng, layers, attention, end):
            layers(eng, 0, False, True)
            with eng.Fori(0, B - 2) as b:
                attention(eng, b, True)
                layers(eng, b + 1, True, True)
            attention(eng, B - 2, True)
            layers(eng, B - 1, True, False)
            attention(eng, B - 1, False)
            if end is not None:
                end(eng, B - 1)

        block = ctx.enter_context(nc.Block())

        @block.sync
        def _(sp):
            sp.dma_start(raw_ww[:], W_w).then_inc(s_const, 16)
            sp.dma_start(raw_a[:], A).then_inc(s_const, 16)
            for i, w in enumerate((W1, W2, W3)):
                sp.dma_start(w_sb[:, i], w).then_inc(s_const, 16)
            for i, row in enumerate(bias_in):
                sp.dma_start(bias[:, i], row.partition_broadcast(P)).then_inc(s_const, 16)
            sp.dma_start(wb_col[:, 0:1], W_b.rearrange("(p o) -> p o", o=1)).then_inc(s_const, 16)
            sp.dma_start(ww_g[:, P:W1G], gate_w[0:P]).then_inc(s_const, 16)
            sp.dma_start(ident_g[:, P:W1G], gate_w[P:2 * P]).then_inc(s_const, 16)
            sp.dma_start(gb[:], gate_b.partition_broadcast(P)).then_inc(s_const, 16)
            load_x(sp, 0, 0)
            load_x(sp, 0, 1)
            for v in range(NV):
                load_stage(sp, 0, 0, v, first=True)
            graphs(sp, sync_layers, sync_attention, sync_end)

        @block.scalar
        def _(act):
            degree_root(act, 0)
            act.wait_ge(s_newton, NEWTON)
            nc.scalar.activation(dinv[:], newton[:], ACT.Copy).then_inc(s_dinv, 1)
            graphs(act, scalar_layers, scalar_attention, scalar_end)

        @block.gpsimd
        def _(pool):
            nc.gpsimd.memset(ones[:], 1.0).then_inc(s_ones, 1)
            nc.gpsimd.memset(ident, 0.0).then_inc(s_ident0, 1)
            pool.wait_ge(s_ident0, 1)
            nc.gpsimd.affine_select(out=ident, in_=ident, compare_op=ALU.not_equal, fill=1.0, base=0,
                                    pattern=[[-1, P]], channel_multiplier=1).then_inc(s_ident, 1)
            graphs(pool, pool_layers, pool_attention, None)

        @block.vector
        def _(dve):
            dve.wait_ge(s_wt, 1)
            nc.vector.tensor_copy(ww_t, bank(0)[:, 0:P]).then_inc(s_wc, 1)
            nc.vector.tensor_tensor(a_sym[:], bank(0)[:, P:2 * P], raw_a[:], ALU.add).then_inc(s_sym, 1)
            dve.wait_ge(s_sw, 1)
            nc.vector.tensor_copy(sw_t[:], bank(1)[:, 0:P]).then_inc(s_swc, 1)
            nc.vector.tensor_copy(wb_col[:, 1:2], bank(1)[:, P:P + 1]).then_inc(s_swc, 1)
            for v in range(NV):
                turn(dve, 0, v)
            first_degrees(dve)
            for i in range(NEWTON):
                newton_step(dve, 0, i)
            graphs(dve, vector_layers, vector_attention, vector_end)

        @block.tensor
        def _(pe):
            pe.wait_ge(s_const, 16 * N_CONST)
            pe.wait_ge(s_ident, 1)
            nc.tensor.transpose(bank(0)[:, 0:P], raw_ww[:], ident)
            nc.tensor.transpose(bank(0)[:, P:2 * P], raw_a[:], ident).then_inc(s_wt, 1)
            pe.wait_ge(s_sym, 1)
            nc.tensor.matmul(bank(1)[:, 0:P], raw_ww[:], a_sym[:], start=True, stop=True)
            nc.tensor.matmul(bank(1)[:, P:P + 1], a_sym[:], wb_col[:, 0:1], start=True,
                             stop=True).then_inc(s_sw, 1)
            pe.wait_ge(s_swc, 2)
            pe.wait_ge(s_ones, 1)
            for t in range(T):
                if t % TG == 0:
                    pe.wait_ge(s_turned, PER_J * (t // TG + 1))
                for g in range(G):
                    last = nc.tensor.matmul(ps_z[g], ones[:], adj_t[:, t, g * CH:(g + 1) * CH],
                                            start=t == 0, stop=t == T - 1)
            last.then_inc(s_degp, 1)
            graphs(pe, tensor_layers, tensor_attention, tensor_end)


_INS = ["x", "adj", "L0_gnn_W1", "L0_gnn_b1", "L0_gnn_W2", "L0_gnn_b2", "L0_gnn_W3", "L0_gnn_b3",
        "L1_gnn_W_w", "L1_gnn_W_b", "L1_gnn_A", "L1_gnn_gate_w", "L1_gnn_gate_b"]


def kernel(**inputs):
    import numpy as _np
    import concourse.bacc as _bacc
    from concourse import mybir as _mybir
    from concourse.bass_utils import run_bass_kernel_spmd as _run

    nc = _bacc.Bacc("TRN2", target_bir_lowering=False, num_devices=1)
    arrays, args = {}, []
    for name in _INS:
        a = _np.ascontiguousarray(inputs[name])
        arrays[f"in_{name}_dram"] = a
        args.append(nc.dram_tensor(f"in_{name}_dram", a.shape, _mybir.dt.from_np(a.dtype), kind="ExternalInput").ap())
    shape = inputs["x"].shape
    args.append(nc.dram_tensor("out_0_dram", shape, _mybir.dt.float32, kind="ExternalOutput").ap())
    gnn_kernel(nc, *args)
    r = _run(nc, [arrays], core_ids=[0])
    return r.results[0]["out_0_dram"]
```

```python
from contextlib import ExitStack

import concourse.bass as bass
from concourse import mybir

ALU = mybir.AluOpType
ACT = mybir.ActivationFunctionType
F32 = mybir.dt.float32
F32R = mybir.dt.float32r
BF16 = mybir.dt.bfloat16

P = 128
N = 2048
Q = 4
C = 32
T = N // P
G = 4
TG = T // G
CH = N // G
L = 3
EPS = 1e-6
NEG = -9000000000000000.0
LOWEST = -3.4e38
ROWS_AT = (12, 13, 15, 17, 18, 19)
END_AT = (17, 19, 20, 24, 26, 27)
W1G = P + 1
GROUPS = [(t, min(t + 3, T)) for t in range(0, T, 3)]
NG = len(GROUPS)
OUT_PARTS = ((0, 3), (3, NG))

NU = L * T * 2
CHUNKS = L * G
HALF = N // 2
ROWS = 256
NB = ROWS // C
NV = (N // ROWS) * G
PER_J = N // ROWS
NSTG = 3
FIRST = 2
NFIRST = 6
WEIGHTS_V = 9
RINGC = 3
DEG_PARTS = 4
PART = N // DEG_PARTS
DEG_UNITS = DEG_PARTS * T
SHARED = (0, 1, 2, 3, T - 2, T - 1)
AHEAD = 7


def unit_order():
    order = []
    for layer in range(L):
        order += [(layer, t, h) for t in range(T - AHEAD) for h in range(2)]
        order += [(layer, t, h) for h in range(2) for t in range(T - AHEAD, T)]
    return order


UNITS = unit_order()
UL = NU // L
RING3 = 19
BUFFER = [(1, 2, 0)[u % 3] if u < RING3 else (1, 2, 0, 3)[u % 4] for u in range(NU)]


LO_MAKER = ("SPSSSSSSSSSSSSSSSSSSVSVPVPVPVPVP"
          "PPPPVPVPVSPVSSVPVPVVSVPVPVVVVPVP"
          "PVPPVPVPVPVPVVPVVSSVVSSPSVVVPVPS")
HI_MAKER = ("AAAAAAAAAAAAAAAAAAAAAAVAAAAAVAAA"
          "VAAAAVAVVAVAAVAVAVVVAAVAVAAVAAVA"
          "VAAAVAVAVAVVAAVVVAAVAVAVAAVAVAVV")
POOL_Q = [{"V": 0, "S": Q // 2, "P": Q}[who] for who in LO_MAKER]
ON_POOL = [q > 0 for q in POOL_Q]
ON_DVE = [q < Q for q in POOL_Q]
HI_ON_DVE = [who == "V" for who in HI_MAKER]
POOL_PER_GRAPH = sum(ON_POOL)
DVE_PER_GRAPH = sum(ON_DVE)
HI_DVE_PER_GRAPH = sum(HI_ON_DVE)
HI_ACT_PER_GRAPH = NU - HI_DVE_PER_GRAPH

EPILOGUE_AT = (3, 5)
MOVE_AT = 30
WEIGHTS_AT = (29, 30)
MOVE_LATE = 3
WEIGHTS_LATE = (0, 1)
SPLIT_AT = 6
BIAS_AT = (2 * UL + 4, 2 * UL + 11, 2 * UL + 19, 2 * UL + 25)
SUM_SPANS = ((1, 2, 32), (2, 4, 29))
SUM_AT = [u for layer, first, end in SUM_SPANS for u in range(layer * UL + first, layer * UL + end)]
SUMMED_BY = {u: DEG_UNITS * (i + 1) // len(SUM_AT) for i, u in enumerate(SUM_AT)}

NEWTON_AT = 5
NEWTON = 5
ROWS_BEFORE = 2
TURN_AT = (2, 5, 7, 9, 11, 13, 15, 18)
TURNS = {t: (2 * (t - TG), 2 * (t - TG) + 1) for t in range(TG, T - 2)}
TURNS[T - 1] = tuple(range(2 * (T - 2 - TG), NV - len(TURN_AT)))
TURNS_LATE = TURNS[T - 1][2:]
X_HALF_AFTER, X_AFTER = 12, 23


def before(u):
    return max((v for v in range(u) if BUFFER[v] == BUFFER[u]), default=None)


def count(u, chosen):
    return sum(1 for v in range(u + 1) if chosen[v])


def last_unit(layer, t):
    return max(u for u, (l, s, _) in enumerate(UNITS) if l == layer and s == t)


def chunk_done(layer, g):
    return max(u for u, (l, _, h) in enumerate(UNITS) if l == layer and h == g // 2)


def stage_count(v, slot):
    return sum(1 for w in range(v + 1) if w % NSTG == slot)


STAGES = [stage_count(NV - 1, s) for s in range(NSTG)]


def gnn_kernel(nc, x, adj, W1, b1, W2, b2, W3, b3, W_w, W_b, A, gate_w, gate_b, out):
    B = x.shape[0]
    nc.disable_value_cache = True

    with ExitStack() as ctx:
        def sem(name):
            return ctx.enter_context(nc.semaphore(name))

        base = (nc.sbuf_base + 63) // 64 * 64
        top = [base]

        def place(nbytes):
            at = top[0]
            top[0] += (nbytes + 31) // 32 * 32
            assert top[0] <= nc.sbuf_usable_end
            return at

        def sb(name, shape, dt, offset):
            return nc.alloc_sbuf_tensor_at(name, shape, dt, offset=offset)

        adj_t = sb("adj_t", [P, T, N], F32, place(T * N * 4))
        blk = [place(N * 4) for _ in range(4)]
        ring0 = place(RINGC * N * 4)
        feat = sb("feat", [P, T, P], F32, blk[0])
        deg_rows = sb("deg_rows", [P, DEG_PARTS, PART], F32, blk[1])
        xs_hi = sb("xs_hi", [P, T, P], F32R, blk[2])
        xs_lo = sb("xs_lo", [P, T, P], F32R, blk[3])
        ut_lo = sb("ut_lo", [P, T, P], F32R, blk[0])
        ht_hi = sb("ht_hi", [P, N], F32R, blk[1])
        ht_lo = sb("ht_lo", [P, N], F32R, blk[2])
        ut_hi = sb("ut_hi", [P, T, P], F32R, blk[3])
        gathered = sb("gathered", [P, T, P], F32, blk[1])
        prob = [sb(f"prob{s}", [P, N], F32, ring0 + s * N * 4) for s in range(RINGC)]
        x4_t = sb("x4_t", [P, T, P], F32, ring0 + 1 * N * 4)
        h_rows = sb("h_rows", [P, T, P], F32, ring0 + 2 * N * 4)
        stage0 = place(NSTG * NB * P * 4)
        stage = [sb(f"stage{s}", [P, NB, P], F32, stage0 + s * NB * P * 4) for s in range(NSTG)]
        first = [sb(f"first{i}", [P, FIRST * NB, P], F32, at)
                 for i, at in enumerate([blk[1], blk[2], blk[3], ring0 + N * 4, ring0 + 2 * N * 4, stage0])]
        pair_sum = sb("pair_sum", [P, N], F32, blk[0])
        pieces = [ring0 + s * N * 4 for s in range(RINGC)] + [stage0]
        a_hi = [sb(f"a_hi{s}", [P, Q, 2 * P], F32R, at) for s, at in enumerate(pieces)]
        a_lo = [sb(f"a_lo{s}", [P, Q, 2 * P], F32R, at + HALF * 4) for s, at in enumerate(pieces)]
        pair0, pair1 = place(CH * 4), place(CH * 4)
        z_sb = [sb("z_sb0", [P, CH], F32, pair0), sb("z_sb1", [P, CH], F32, pair1)]
        x4_back = [sb("x4_back0", [P, CH], F32, pair0), sb("x4_back1", [P, CH], F32, pair1)]
        mask = [sb("mask0", [P, HALF], BF16, pair0), sb("mask1", [P, HALF], BF16, pair1)]
        h_in = [sb(f"h_in{s}", [P, P], F32, place(P * 4)) for s in range(2)]
        ones = sb("ones", [P, P], F32, top[0] - 2 * P * 4)
        diag = sb("diag", [P, T, Q, C], F32, ring0 + 2 * N * 4)
        h_norm = [sb(f"h_norm{s}", [P, P], F32, place(P * 4)) for s in range(2)]
        w_sb = sb("w_sb", [P, L, P], F32, place(L * P * 4))
        ww_g = sb("ww_g", [P, W1G], F32, place(W1G * 4))
        sw_t = sb("sw_t", [P, P], F32, place(P * 4))
        ident_g = sb("ident_g", [P, W1G], F32, place(W1G * 4))
        ident, ww_t = ident_g[:, 0:P], ww_g[:, 0:P]
        bias = sb("bias", [P, L + 1, P], F32, place((L + 1) * P * 4))
        columns = sb("columns", [P, 14 + 10 * T], F32, place((14 + 10 * T) * 4))
        taken = [0]

        def cols(n):
            taken[0] += n
            return columns[:, taken[0] - n:taken[0]]

        wb_col = cols(2)
        gb = cols(1)
        deg_part = cols(DEG_PARTS * T).rearrange("p (t h) -> p t h", h=DEG_PARTS)
        deg, root, newton, dinv = cols(T), cols(T), cols(T), cols(T)
        top_half, top_full, neg_top, total, inv_total = ([cols(1), cols(1)] for _ in range(5))
        coef_x, coef = cols(T), cols(T)
        warm = cols(1)
        raw_ww = sb("raw_ww", [P, P], F32, ring0)
        raw_a = sb("raw_a", [P, P], F32, ring0 + P * 4)
        a_sym = sb("a_sym", [P, P], F32, ring0 + 2 * P * 4)

        ps_all = ctx.enter_context(nc.psum_tensor("ps_z", [P, N], F32))
        ps_z = [ps_all[:, g * CH:(g + 1) * CH] for g in range(G)]
        ps_e = ctx.enter_context(nc.psum_tensor("ps_e", [P, N], F32))

        def bank(g):
            return ps_e[:, g * CH:(g + 1) * CH]

        x4_dram = nc.dram_tensor("x4_dram", (P, N), F32, kind="Internal").ap()
        h_dram = nc.dram_tensor("h_dram", (P, N), F32, kind="Internal").ap()

        s_const = sem("s_const")
        s_ident0, s_ident = sem("s_ident0"), sem("s_ident")
        s_wt, s_sym, s_wc, s_sw, s_swc = sem("s_wt"), sem("s_sym"), sem("s_wc"), sem("s_sw"), sem("s_swc")
        s_x = [sem(f"s_x{i}") for i in range(2)]
        s_rows = [sem(f"s_rows{s}") for s in range(DEG_PARTS)]
        s_deg = sem("s_deg")
        s_degadd = sem("s_degadd")
        s_dsum, s_root, s_newton, s_dinv = sem("s_dsum"), sem("s_root"), sem("s_newton"), sem("s_dinv")
        s_stage = [sem(f"s_stage{s}") for s in range(NSTG)]
        s_first = [sem(f"s_first{s}") for s in range(NFIRST)]
        s_pair, s_paired = sem("s_pair"), sem("s_paired")
        s_turned = sem("s_turned")
        s_hi_act, s_hi_dve = sem("s_hi_act"), sem("s_hi_dve")
        s_lo_dve, s_lo_pool = sem("s_lo_dve"), sem("s_lo_pool")
        s_unit = sem("s_unit")
        s_zsb, s_zw, s_affine, s_h = sem("s_zsb"), sem("s_zw"), sem("s_affine"), sem("s_h")
        s_hb = sem("s_hb")
        s_xhi, s_xlo = sem("s_xhi"), sem("s_xlo")
        s_spill = [sem(f"s_spill{g}") for g in range(G)]
        s_xt, s_xtc = sem("s_xt"), sem("s_xtc")
        s_ht, s_hthi, s_htlo = sem("s_ht"), sem("s_hthi"), sem("s_htlo")
        s_ut, s_uthi, s_utlo = sem("s_ut"), sem("s_uthi"), sem("s_utlo")
        s_hr, s_hrc, s_hrb = sem("s_hr"), sem("s_hrc"), sem("s_hrb")
        s_hspill = [sem(f"s_hspill{i}") for i in range(NG)]
        s_e = sem("s_e")
        s_mask, s_top, s_neg = sem("s_mask"), sem("s_top"), sem("s_neg")
        s_exp, s_prob, s_prob_dve = sem("s_exp"), sem("s_prob"), sem("s_prob_dve")
        s_inv, s_hnorm = sem("s_inv"), sem("s_hnorm")
        s_hin = [sem(f"s_hin{s}") for s in range(2)]
        s_pv = sem("s_pv")
        s_rel_act, s_rel_dve = sem("s_rel_act"), sem("s_rel_dve")
        s_coef, s_gt, s_minus = sem("s_coef"), sem("s_gt"), sem("s_minus")
        s_back = [sem(f"s_back{s}") for s in range(2)]
        s_diff = sem("s_diff")
        s_out = sem("s_out")
        s_ones, s_newton0 = sem("s_ones"), sem("s_newton0")

        s_met_dve, s_met_sp = sem("s_met_dve"), sem("s_met_sp")

        def natural(ap, g):
            return ap.rearrange("p (q g x) -> p g q x", q=Q, g=G)[:, g]

        def chunk_of_unit(buf, g):
            return buf[:, :, (g % 2) * P:(g % 2 + 1) * P]

        def half_columns(t, h):
            return adj_t[:, t].rearrange("p (q h x) -> p h q x", q=Q, h=2)[:, h]

        def by_tile(ap):
            return ap.rearrange("p (q s c) -> p q s c", q=Q, s=TG)

        def tile_major(ap):
            return ap.rearrange("p (s q c) -> p q s c", q=Q, s=TG)

        def by_quadrant(ap):
            return ap.rearrange("p (q x) -> p q x", q=Q)

        def tiles(buf, g):
            return buf[:, g * TG:(g + 1) * TG].rearrange("p s f -> p (s f)")

        def node_rows(dram, quadrant, t0, t1):
            per = N // Q
            return dram[quadrant * per + t0 * C:quadrant * per + t1 * C].rearrange("(t c) f -> c t f", c=C)

        def group(bank_ap, n):
            wide = bank_ap[:, 0:n * W1G].rearrange("p (s f) -> p s f", f=W1G)
            return wide[:, :, 0:P], bank_ap[:, P:n * W1G:W1G]

        bias_in = [b1, b2, b3, W_b]
        N_CONST = 5 + len(bias_in) + 4

        def settle(eng, passed):
            eng.sem_inc(passed, 1)

        OUT_INC = 16 * Q * len(OUT_PARTS)

        def load_x(sp, b, half):
            t0, t1 = half * T // 2, (half + 1) * T // 2
            for q in range(Q):
                sp.dma_start(feat[q * C:(q + 1) * C, t0:t1], node_rows(x[b], q, t0, t1)).then_inc(s_x[half], 16)

        def load_rows(sp, b):
            for d in range(DEG_UNITS):
                t, h = d // DEG_PARTS, d % DEG_PARTS
                if t > 0:
                    sp.wait_ge(s_deg, DEG_UNITS * b + d - DEG_PARTS + 1)
                sp.dma_start(deg_rows[:, h], adj[b + 1, t * P:(t + 1) * P, h * PART:(h + 1) * PART]
                             ).then_inc(s_rows[h], 16)

        def first_part(v):
            J, r = v // (PER_J // FIRST), v % (PER_J // FIRST)
            return J * TG, slice(r * FIRST * ROWS, (r + 1) * FIRST * ROWS)

        def load_first(sp, v):
            if v >= NFIRST:
                sp.wait_ge(s_turned, FIRST * (v - NFIRST + 1))
            t, rows = first_part(v)
            for q in range(Q):
                col = q * (N // Q) + t * C
                src = adj[0, rows, col:col + P].rearrange("(n c) j -> c n j", c=C)
                sp.dma_start(first[v % NFIRST][q * C:(q + 1) * C], src).then_inc(s_first[v % NFIRST], 16)

        def load_stage(sp, b, k, v):
            sp.wait_ge(s_turned, NV * k + max(v - NSTG + 1, 0))
            J, r = v // (N // ROWS), v % (N // ROWS)
            for q in range(Q):
                col = q * (N // Q) + J * P
                src = adj[b, r * ROWS:(r + 1) * ROWS, col:col + P].rearrange("(n c) j -> c n j", c=C)
                sp.dma_start(stage[v % NSTG][q * C:(q + 1) * C], src).then_inc(s_stage[v % NSTG], 16)

        def sync_end(sp, b):
            sp.wait_ge(s_top, 2 * T * b + 2 * T)
            for i, (t0, t1) in enumerate(GROUPS):
                if i >= 2:
                    sp.wait_ge(s_diff, NG * b + i - 1)
                sp.dma_start(x4_back[i % 2][:, 0:(t1 - t0) * P], x4_dram[:, t0 * P:t1 * P]).then_inc(s_back[i % 2], 16)
            for i0, i1 in OUT_PARTS:
                sp.wait_ge(s_diff, NG * b + i1)
                t0, t1 = GROUPS[i0][0], GROUPS[i1 - 1][1]
                for q in range(Q):
                    sp.dma_start(node_rows(out[b], q, t0, t1), gathered[q * C:(q + 1) * C, t0:t1]).then_inc(s_out, 16)
            sp.wait_ge(s_out, OUT_INC * b + OUT_INC)

        def sync_layers(sp, b, end, more):
            if end:
                sync_end(sp, b - 1)
            else:
                sp.wait_ge(s_turned, NV)
            if more:
                load_rows(sp, b)
            for g in range(G):
                sp.wait_ge(s_h, CHUNKS * b + 2 * G + g + 1)
                sp.dma_start(x4_dram[:, g * CH:(g + 1) * CH], tiles(feat, g)).then_inc(s_spill[g], 16)
            for i, (t0, t1) in enumerate(GROUPS):
                sp.wait_ge(s_hrb, NG * b + i + 1)
                sp.dma_start(h_dram[:, t0 * P:t1 * P],
                             h_rows[:, t0:t1].rearrange("p t f -> p (t f)")).then_inc(s_hspill[i], 16)

        def sync_attention(sp, b, more):
            if more:
                for v in range(NV):
                    load_stage(sp, b + 1, b + 1, v)
                    if v == X_HALF_AFTER:
                        sp.wait_ge(s_e, 2 * T * b + T)
                        load_x(sp, b + 1, 0)
                    if v == X_AFTER:
                        sp.wait_ge(s_e, 2 * T * b + 2 * T)
                        load_x(sp, b + 1, 1)
            settle(sp, s_met_sp)

        def sum_rows(act, b, d):
            t, h = d // DEG_PARTS, d % DEG_PARTS
            act.wait_ge(s_rows[h], 16 * T * b + 16 * (t + 1))
            nc.scalar.activation(deg_rows[:, h], deg_rows[:, h], ACT.Copy,
                                 accum_out=deg_part[:, t, h:h + 1]).then_inc(s_deg, 1)

        def dinv_by_node(act, k, q):
            act.wait_ge(s_newton, NEWTON * k + NEWTON)
            for s in range(TG):
                last = nc.scalar.activation(dinv[q * C:(q + 1) * C, s:T:TG],
                                            newton[s * C:(s + 1) * C, q * G:(q + 1) * G], ACT.Copy)
            if q == Q - 1:
                last.then_inc(s_dinv, 1)

        def degree_root(act, k):
            act.wait_ge(s_dsum, k + 1)
            nc.scalar.activation(root[:], deg[:], ACT.Sqrt).then_inc(s_root, 1)

        def split_x(act, b, end, layer, t):
            if layer == 0 and t % (T // 2) == 0:
                act.wait_ge(s_x[t // (T // 2)], 16 * Q * b + 16 * Q)
            if layer == 0 and t == 0:
                act.wait_ge(s_dinv, b + 1)
                if end:
                    act.wait_ge(s_e, 2 * T * b)
            elif layer > 0:
                act.wait_ge(s_h, CHUNKS * b + (layer - 1) * G + t // TG + 1)
                act.wait_ge(s_unit, NU * b + last_unit(layer - 1, t) + 1)
            nc.scalar.activation(xs_hi[:, t], feat[:, t], ACT.Copy, scale=dinv[:, t:t + 1]).then_inc(s_xhi, 1)

        def wait_buffer(eng, b, end, u):
            layer, t, _ = UNITS[u]
            if before(u) is not None:
                eng.wait_ge(s_unit, NU * b + before(u) + 1)
            elif BUFFER[u] < RINGC and end:
                eng.wait_ge(s_pv, T * b - RINGC + 1 + u)
            if layer == 0:
                eng.wait_ge(s_turned, NV * b + (NV if BUFFER[u] == RINGC else PER_J * (t // TG) + PER_J))

        def make_hi(act, b, end, u):
            layer, t, h = UNITS[u]
            wait_buffer(act, b, end, u)
            nc.scalar.activation(a_hi[BUFFER[u]][:], half_columns(t, h), ACT.Copy).then_inc(s_hi_act, 1)

        def move_z(act, b, end, layer, g):
            i = layer * G + g
            act.wait_ge(s_unit, NU * b + chunk_done(layer, g) + 1)
            if i == 0 and end:
                act.wait_ge(s_diff, NG * b)
            if i >= 2:
                act.wait_ge(s_zw, CHUNKS * b + i - 1)
            nc.scalar.activation(tile_major(z_sb[g % 2][:]), by_tile(ps_z[g]), ACT.Copy).then_inc(s_zsb, 1)

        def scalar_end(act, b):
            act.wait_ge(s_pv, T * b + T)
            for g in range(0, G, 2):
                nc.scalar.activation(tile_major(tiles(gathered, g)), by_tile(ps_z[g]), ACT.Relu).then_inc(s_rel_act, 1)

        def scalar_layers(act, b, end, more):
            summed = 0
            for u in range(NU):
                layer, since = UNITS[u][0], u % UL
                if layer == 0:
                    if since == 0:
                        split_x(act, b, end, 0, 0)
                    if since == 2 and end:
                        scalar_end(act, b - 1)
                    if 2 <= since < T + 1:
                        split_x(act, b, end, 0, since - 1)
                else:
                    if since == 2:
                        for t in range(TG):
                            split_x(act, b, end, layer, t)
                    if since == MOVE_LATE:
                        move_z(act, b, end, layer - 1, 2)
                        move_z(act, b, end, layer - 1, 3)
                    if 0 <= since - SPLIT_AT < T - TG:
                        split_x(act, b, end, layer, since - SPLIT_AT + TG)
                if since == MOVE_AT:
                    move_z(act, b, end, layer, 0)
                    move_z(act, b, end, layer, 1)
                if not HI_ON_DVE[u]:
                    make_hi(act, b, end, u)
                while more and summed < SUMMED_BY.get(u, 0):
                    sum_rows(act, b, summed)
                    summed += 1
            move_z(act, b, end, L - 1, 2)
            move_z(act, b, end, L - 1, 3)

            def transposed(g):
                act.wait_ge(s_xt, G * b + g + 1)
                nc.scalar.activation(tiles(x4_t, g), ps_z[g], ACT.Copy).then_inc(s_xtc, 1)

            def h_transposed(g):
                act.wait_ge(s_ht, G * b + g + 1)
                if g == 0 and not more:
                    act.wait_ge(s_out, OUT_INC * b)
                nc.scalar.activation(natural(ht_hi[:], g), by_quadrant(bank(g)), ACT.Identity,
                                     bias=wb_col[:, 0:1]).then_inc(s_hthi, 1)

            transposed(0)
            for g in range(G):
                if g + 1 < G:
                    transposed(g + 1)
                h_transposed(g)
                act.wait_ge(s_ut, G * b + g + 1)
                nc.scalar.activation(tiles(ut_hi, g), ps_z[g][:], ACT.Identity,
                                     bias=wb_col[:, 1:2]).then_inc(s_uthi, 1)

        def scalar_attention(act, b, more):
            def load_h(t):
                act.wait_ge(s_hspill[t // 3], 16 * b + 16)
                if t >= 3:
                    act.wait_ge(s_hnorm, T * b + t - 1)
                act.dma_start(h_in[t % 2][:], h_dram[:, t * P:(t + 1) * P]).then_inc(s_hin[t % 2], 16)

            def normalize(t):
                if t > 0:
                    act.wait_ge(s_hin[t % 2], 16 * (T // 2 - 1 + t % 2) * b + 16 * ((t + 1) // 2))
                act.wait_ge(s_inv, T * b + t + 1)
                if t == 0:
                    act.wait_ge(s_hrb, NG * b + 1)
                if t >= 2:
                    act.wait_ge(s_pv, T * b + t - 1)
                nc.scalar.activation(h_norm[t % 2][:], h_rows[:, 0] if t == 0 else h_in[t % 2][:], ACT.Copy,
                                     scale=inv_total[t % 2][:]).then_inc(s_hnorm, 1)
                if 0 < t and t + 2 < T:
                    load_h(t + 2)

            if more:
                degree_root(act, b + 1)
                nc.scalar.activation(warm[:], wb_col[:, 0:1], ACT.Exp)
            for i, (t0, t1) in enumerate(GROUPS):
                act.wait_ge(s_hr, NG * b + i + 1)
                rows, gates = group(ps_z[i % G], t1 - t0)
                nc.scalar.activation(h_rows[:, t0:t1], rows, ACT.Copy)
                nc.scalar.activation(coef_x[:, t0:t1], gates, ACT.Copy).then_inc(s_hrc, 1)
            for t in range(T):
                act.wait_ge(s_top, 2 * T * b + 2 * t + 2)
                if t >= 2:
                    act.wait_ge(s_exp, T * b + t - 1)
                nc.scalar.activation(neg_top[t % 2][:], top_full[t % 2][:], ACT.Copy,
                                     scale=-1.0).then_inc(s_neg, 1)
                act.wait_ge(s_neg, T * b + t + 1)
                if t >= 2:
                    act.wait_ge(s_inv, T * b + t - 1)
                nc.scalar.activation(prob[t % RINGC][:], prob[t % RINGC][:], ACT.Exp, bias=neg_top[t % 2][:],
                                     accum_out=total[t % 2][:]).then_inc(s_exp, 1)
                normalize(t)
                if t == 0:
                    load_h(1)
                    load_h(2)
                if more and 0 <= t - NEWTON_AT - NEWTON < Q:
                    dinv_by_node(act, b + 1, t - NEWTON_AT - NEWTON)

        def turn_first(dve, v):
            t, rows = first_part(v)
            dve.wait_ge(s_first[v % NFIRST], 16 * Q * (v // NFIRST + 1))
            dst = adj_t[:, t:t + TG, rows].rearrange("p t (n r) -> p t n r", r=C)
            src = first[v % NFIRST][:].rearrange("p n (t c) -> p t n c", t=TG)
            nc.vector.transpose(dst, src).then_inc(s_turned, FIRST)

        def turn(dve, k, v):
            J, r = v // (N // ROWS), v % (N // ROWS)
            slot = v % NSTG
            dve.wait_ge(s_stage[slot], 16 * Q * (STAGES[slot] * (k - 1) + stage_count(v, slot)))
            dst = adj_t[:, J * TG:(J + 1) * TG, r * ROWS:(r + 1) * ROWS].rearrange("p t (n r) -> p t n r", r=C)
            src = stage[slot][:].rearrange("p n (t c) -> p t n c", t=TG)
            nc.vector.transpose(dst, src).then_inc(s_turned, 1)

        def degrees(dve, b):
            dve.wait_ge(s_deg, DEG_UNITS * b + DEG_UNITS)
            nc.vector.scalar_tensor_tensor(out=deg[:], in0=deg_part[:, :, 0], scalar=EPS, in1=deg_part[:, :, 1],
                                           op0=ALU.add, op1=ALU.add).then_inc(s_degadd, 1)
            nc.vector.tensor_tensor(newton[:], deg_part[:, :, 2], deg_part[:, :, 3], ALU.add).then_inc(s_degadd, 1)
            dve.wait_ge(s_degadd, 2 * b + 2)
            nc.vector.tensor_tensor(deg[:], deg[:], newton[:], ALU.add).then_inc(s_dsum, 1)

        def first_degrees(dve):
            dve.wait_ge(s_paired, NV // FIRST)
            dve.wait_ge(s_ident, 1)
            row = ps_all[:].rearrange("p (q t c) -> p t q c", q=Q, c=C)
            for t in range(T):
                nc.vector.tensor_tensor_reduce(
                    out=diag[:, t], in0=row[:, t], in1=ident.rearrange("p (q c) -> p q c", q=Q), scale=1.0,
                    scalar=EPS, op0=ALU.mult, op1=ALU.add, accum_out=deg[:, t:t + 1]).then_inc(s_newton0, 1)
            dve.wait_ge(s_newton0, T)
            dve.sem_inc(s_dsum, 1)

        def newton_step(dve, k, i):
            if i == 0:
                dve.wait_ge(s_root, k + 1)
                nc.vector.reciprocal(root[:], root[:]).then_inc(s_newton, 1)
                return
            dve.wait_ge(s_newton, NEWTON * k + i)
            if i == 1:
                nc.vector.tensor_tensor(newton[:], root[:], root[:], ALU.mult).then_inc(s_newton, 1)
            elif i == 2:
                nc.vector.tensor_tensor(newton[:], newton[:], deg[:], ALU.mult).then_inc(s_newton, 1)
            elif i == 3:
                nc.vector.tensor_scalar(newton[:], newton[:], -0.5, 1.5, ALU.mult, ALU.add).then_inc(s_newton, 1)
            else:
                nc.vector.tensor_tensor(newton[:], newton[:], root[:], ALU.mult).then_inc(s_newton, 1)

        def split_x_lo(dve, b, layer, t):
            dve.wait_ge(s_xhi, L * T * b + layer * T + t + 1)
            nc.vector.scalar_tensor_tensor(out=xs_lo[:, t], in0=feat[:, t], scalar=dinv[:, t:t + 1],
                                           in1=xs_hi[:, t].bitcast(F32), op0=ALU.mult,
                                           op1=ALU.subtract).then_inc(s_xlo, 1)

        def make_hi_dve(dve, b, end, u):
            _, t, h = UNITS[u]
            wait_buffer(dve, b, end, u)
            nc.vector.tensor_copy(a_hi[BUFFER[u]][:], half_columns(t, h)).then_inc(s_hi_dve, 1)

        def make_lo(eng, ops, b, u, signal):
            _, t, h = UNITS[u]
            if HI_ON_DVE[u]:
                eng.wait_ge(s_hi_dve, HI_DVE_PER_GRAPH * b + count(u, HI_ON_DVE))
            else:
                eng.wait_ge(s_hi_act, HI_ACT_PER_GRAPH * b + u + 1 - count(u, HI_ON_DVE))
            part = slice(0, POOL_Q[u]) if signal is s_lo_pool else slice(POOL_Q[u], Q)
            ops.tensor_tensor(a_lo[BUFFER[u]][:, part], half_columns(t, h)[:, part],
                              a_hi[BUFFER[u]][:, part].bitcast(F32), ALU.subtract).then_inc(signal, 1)

        def epilogue(dve, b, layer, g):
            i = CHUNKS * b + layer * G + g
            dve.wait_ge(s_zw, i + 1)
            if layer == L - 1:
                dve.wait_ge(s_hb, G * b + g + 1)
                for s in range(TG):
                    t = g * TG + s
                    last = nc.vector.scalar_tensor_tensor(out=feat[:, t], in0=bank(g)[:, s * P:(s + 1) * P],
                                                          scalar=dinv[:, t:t + 1], in1=feat[:, t],
                                                          op0=ALU.mult, op1=ALU.add)
                last.then_inc(s_h, 1)
                return
            for s in range(TG):
                t = g * TG + s
                yp = bank(g)[:, s * P:(s + 1) * P]
                last = nc.vector.scalar_tensor_tensor(out=yp, in0=yp, scalar=dinv[:, t:t + 1],
                                                      in1=bias[:, layer], op0=ALU.mult, op1=ALU.add)
            last.then_inc(s_affine, 1)
            dve.wait_ge(s_affine, (L - 1) * G * b + layer * G + g + 1)
            nc.vector.scalar_tensor_tensor(out=tiles(feat, g), in0=bank(g), scalar=0.0, in1=tiles(feat, g),
                                           op0=ALU.max, op1=ALU.add).then_inc(s_h, 1)

        def end_group(dve, b, i):
            t0, t1 = GROUPS[i]
            n = t1 - t0
            dve.wait_ge(s_gt, NG * b + i + 1)
            rows, gates = group(bank(i % G), n)
            nc.vector.scalar_tensor_tensor(out=coef[:, t0:t1], in0=gates, scalar=gb[:], in1=coef_x[:, t0:t1],
                                           op0=ALU.add, op1=ALU.add).then_inc(s_coef, 1)
            dve.wait_ge(s_back[i % 2], 16 * (NG // 2) * b + 16 * (i // 2 + 1))
            back = x4_back[i % 2][:, 0:n * P].rearrange("p (s f) -> p s f", f=P)
            nc.vector.tensor_tensor(back, back, rows, ALU.subtract).then_inc(s_minus, 1)
            dve.wait_ge(s_coef, NG * b + i + 1)
            dve.wait_ge(s_minus, NG * b + i + 1)
            for s in range(n):
                last = nc.vector.scalar_tensor_tensor(out=gathered[:, t0 + s], in0=back[:, s],
                                                      scalar=coef[:, t0 + s:t0 + s + 1], in1=rows[:, s],
                                                      op0=ALU.mult, op1=ALU.add)
            last.then_inc(s_diff, 1)

        def relu_gathered(dve, b):
            dve.wait_ge(s_pv, T * b + T)
            for g in range(1, G, 2):
                for s in range(TG):
                    last = nc.vector.tensor_scalar(
                        gathered[:, g * TG + s].rearrange("p (q c) -> p q c", q=Q),
                        ps_z[g].rearrange("p (q s c) -> p s q c", q=Q, s=TG)[:, s], 0.0, None, ALU.max)
                last.then_inc(s_rel_dve, 1)

        def vector_end(dve, b):
            relu_gathered(dve, b)
            for i in range(NG):
                end_group(dve, b, i)

        def vector_layers(dve, b, end, more):
            for u in range(NU):
                layer, since = UNITS[u][0], u % UL
                if layer == 0:
                    if end and since in TURN_AT:
                        turn(dve, b, NV - len(TURN_AT) + TURN_AT.index(since))
                    if since == 0:
                        split_x_lo(dve, b, 0, 0)
                    if since == 1 and end:
                        relu_gathered(dve, b - 1)
                    if 1 <= since < T:
                        split_x_lo(dve, b, 0, since)
                    if end and since in END_AT:
                        end_group(dve, b - 1, END_AT.index(since))
                else:
                    if since == 0:
                        epilogue(dve, b, layer - 1, 0)
                        for t in range(TG):
                            split_x_lo(dve, b, layer, t)
                        epilogue(dve, b, layer - 1, 1)
                    if since in EPILOGUE_AT:
                        epilogue(dve, b, layer - 1, 2 + EPILOGUE_AT.index(since))
                    if 0 <= since - SPLIT_AT < T - TG:
                        split_x_lo(dve, b, layer, since - SPLIT_AT + TG)
                if u + 1 < NU and HI_ON_DVE[u + 1]:
                    make_hi_dve(dve, b, end, u + 1)
                if ON_DVE[u]:
                    make_lo(dve, nc.vector, b, u, s_lo_dve)
            for g in range(G):
                epilogue(dve, b, L - 1, g)
            if more:
                degrees(dve, b)
            for g in range(G):
                dve.wait_ge(s_hthi, G * b + g + 1)
                nc.vector.scalar_tensor_tensor(
                    out=natural(ht_lo[:], g), in0=by_quadrant(bank(g)), scalar=wb_col[:, 0:1],
                    in1=natural(ht_hi[:], g).bitcast(F32),
                    op0=ALU.add, op1=ALU.subtract).then_inc(s_htlo, 1)
                dve.wait_ge(s_uthi, G * b + g + 1)
                dve.wait_ge(s_spill[g], 16 * b + 16)
                nc.vector.scalar_tensor_tensor(out=tiles(ut_lo, g), in0=ps_z[g], scalar=wb_col[:, 1:2],
                                               in1=tiles(ut_hi, g).bitcast(F32), op0=ALU.add,
                                               op1=ALU.subtract).then_inc(s_utlo, 1)

        def vector_attention(dve, b, more):
            def inverse_total(t):
                dve.wait_ge(s_exp, T * b + t + 1)
                if t >= 2:
                    dve.wait_ge(s_hnorm, T * b + t - 1)
                nc.vector.reciprocal(inv_total[t % 2][:], total[t % 2][:]).then_inc(s_inv, 1)

            def make_mask(t, h):
                if t > 0:
                    dve.wait_ge(s_top, 2 * T * b + 2 * t + h - 1)
                else:
                    dve.wait_ge(s_zw, CHUNKS * (b + 1) - 1 + h)
                nc.vector.tensor_scalar(mask[h][:], adj_t[:, t, h * HALF:(h + 1) * HALF], 0.0, NEG, ALU.is_le,
                                        ALU.mult).then_inc(s_mask, 1)

            def mask_scores(t, h):
                cols = slice(h * HALF, (h + 1) * HALF)
                dve.wait_ge(s_mask, 2 * T * b + 2 * t + h + 1)
                dve.wait_ge(s_e, 2 * T * b + 2 * t + h + 1)
                if h == 1:
                    dve.wait_ge(s_top, 2 * T * b + 2 * t + 1)
                settle(dve, s_met_dve)
                nc.vector.tensor_tensor_reduce(
                    out=prob[t % RINGC][:, cols], in0=ps_e[:, cols], in1=mask[h][:], scale=1.0,
                    scalar=LOWEST if h == 0 else top_half[t % 2][:], op0=ALU.add, op1=ALU.max,
                    accum_out=(top_half if h == 0 else top_full)[t % 2][:]).then_inc(s_top, 1)

            def end_exp(t):
                inverse_total(t)
                if t in SHARED:
                    nc.vector.tensor_tensor(prob[t % RINGC][:, HALF:], prob[t % RINGC][:, HALF:],
                                            adj_t[:, t, HALF:], ALU.mult).then_inc(s_prob_dve, 1)

            def turn_next(v):
                if v % PER_J == 0:
                    dve.wait_ge(s_prob, T * b + TG * (v // PER_J) + TG)
                turn(dve, b + 1, v)

            late = [t for t in range(T - 1) if not more or t < TG or t == T - 2]
            make_mask(0, 0)
            make_mask(0, 1)
            for t in range(T):
                if t == 2:
                    for i in range(NG):
                        dve.wait_ge(s_hspill[i], 16 * b + 16)
                    dve.wait_ge(s_hnorm, T * b + 1)
                if t == 1:
                    dve.wait_ge(s_hr, NG * b + NG)
                if t >= RINGC:
                    dve.wait_ge(s_pv, T * b + t - RINGC + 1)
                if t >= 2:
                    dve.wait_ge(s_neg, T * b + t - 1)
                mask_scores(t, 0)
                mask_scores(t, 1)
                if t - 1 in late:
                    end_exp(t - 1)
                stagings = [v for v in TURNS.get(t, ()) if v not in TURNS_LATE] if more else []
                for h in range(2):
                    if t + 1 < T:
                        make_mask(t + 1, h)
                    for v in stagings[h:h + 1]:
                        turn_next(v)
                if more and 0 <= t - NEWTON_AT < NEWTON:
                    newton_step(dve, b + 1, t - NEWTON_AT)
                if t not in late:
                    end_exp(t)
            if more:
                for v in TURNS_LATE:
                    turn_next(v)

        def gather_unit(pe, b, end, u):
            layer, t, h = UNITS[u]
            if h == 0:
                pe.wait_ge(s_xlo, L * T * b + layer * T + t + 1)
            if t == 0 and layer > 0:
                pe.wait_ge(s_zsb, CHUNKS * b + (layer - 1) * G + 2 * h + 2)
            elif t == 0 and end:
                pe.wait_ge(s_rel_act, 2 * b - 1 + h)
                pe.wait_ge(s_rel_dve, 2 * b - 1 + h)
            if ON_POOL[u]:
                pe.wait_ge(s_lo_pool, POOL_PER_GRAPH * b + count(u, ON_POOL))
            if ON_DVE[u]:
                pe.wait_ge(s_lo_dve, DVE_PER_GRAPH * b + count(u, ON_DVE))
            hi, lo = a_hi[BUFFER[u]], a_lo[BUFFER[u]]
            pair = (2 * h, 2 * h + 1)
            for g in pair:
                nc.tensor.matmul(ps_z[g], xs_lo[:, t], chunk_of_unit(hi, g), start=t == 0, stop=False)
            for g in pair:
                nc.tensor.matmul(ps_z[g], xs_hi[:, t], chunk_of_unit(hi, g), start=False, stop=False)
            for g in pair:
                last = nc.tensor.matmul(ps_z[g], xs_hi[:, t], chunk_of_unit(lo, g), start=False,
                                        stop=t == T - 1)
            last.then_inc(s_unit, 1)

        def weight_z(pe, b, end, layer, g):
            pe.wait_ge(s_zsb, CHUNKS * b + layer * G + g + 1)
            if layer > 0:
                pe.wait_ge(s_h, CHUNKS * b + (layer - 1) * G + g + 1)
            elif end and g == 0:
                pe.wait_ge(s_diff, NG * b)
            for s in range(TG):
                last = nc.tensor.matmul(bank(g)[:, s * P:(s + 1) * P], z_sb[g % 2][:, s * P:(s + 1) * P],
                                        w_sb[:, layer], start=True, stop=True)
            last.then_inc(s_zw, 1)

        def rows_of_gathered(pe, b, i):
            t0, t1 = GROUPS[i]
            if i == 0:
                pe.wait_ge(s_rel_act, 2 * b + 2)
                pe.wait_ge(s_rel_dve, 2 * b + 2)
                pe.wait_ge(s_top, 2 * T * b + 2 * T)
            if i >= G:
                pe.wait_ge(s_diff, NG * b + i - G + 1)
            for s in range(t1 - t0):
                last = nc.tensor.matmul(bank(i % G)[:, s * W1G:(s + 1) * W1G], gathered[:, t0 + s], ident_g[:],
                                        start=True, stop=True)
            last.then_inc(s_gt, 1)

        def tensor_end(pe, b):
            for i in range(NG):
                rows_of_gathered(pe, b, i)

        def tensor_layers(pe, b, end, more):
            for u in range(NU):
                layer, since = UNITS[u][0], u % UL
                if since in WEIGHTS_AT:
                    weight_z(pe, b, end, layer, WEIGHTS_AT.index(since))
                gather_unit(pe, b, end, u)
                for g in range(2, G):
                    if layer > 0 and since == WEIGHTS_LATE[g - 2]:
                        weight_z(pe, b, end, layer - 1, g)
                if end and u in ROWS_AT:
                    rows_of_gathered(pe, b - 1, ROWS_AT.index(u))

            def transpose_x(g):
                pe.wait_ge(s_h, CHUNKS * b + 2 * G + g + 1)
                for s in range(TG):
                    last = nc.tensor.transpose(ps_z[g][:, s * P:(s + 1) * P], feat[:, g * TG + s], ident)
                last.then_inc(s_xt, 1)

            weight_z(pe, b, end, L - 1, 2)
            transpose_x(0)
            weight_z(pe, b, end, L - 1, 3)
            for g in range(G):
                if g + 1 < G:
                    transpose_x(g + 1)
                pe.wait_ge(s_xtc, G * b + g + 1)
                nc.tensor.matmul(bank(g), ww_t, tile_major(tiles(x4_t, g)), start=True, stop=True).then_inc(s_ht, 1)
                nc.tensor.matmul(ps_z[g], sw_t[:], tiles(x4_t, g), start=True, stop=True).then_inc(s_ut, 1)

        def tensor_attention(pe, b, more):
            def rows_of_h(i):
                t0, t1 = GROUPS[i]
                if i < G:
                    pe.wait_ge(s_utlo, G * b + i + 1)
                else:
                    pe.wait_ge(s_hrc, NG * b + i - G + 1)
                for s in range(t1 - t0):
                    last = nc.tensor.matmul(ps_z[i % G][:, s * W1G:(s + 1) * W1G], x4_t[:, t0 + s], ww_g[:],
                                            start=True, stop=True)
                last.then_inc(s_hr, 1)

            def scores(t):
                if t % TG == 0:
                    pe.wait_ge(s_utlo, G * b + t // TG + 1)
                if t == 0:
                    pe.wait_ge(s_htlo, G * b + G)
                for h in range(2):
                    if t > 0:
                        pe.wait_ge(s_top, 2 * T * b + 2 * t - 1 + h)
                    banks = (2 * h, 2 * h + 1)
                    for g in banks:
                        nc.tensor.matmul(bank(g), ut_lo[:, t], ht_hi[:, g * CH:(g + 1) * CH], start=True, stop=False)
                    for g in banks:
                        nc.tensor.matmul(bank(g), ut_hi[:, t], ht_hi[:, g * CH:(g + 1) * CH], start=False, stop=False)
                    for g in banks:
                        last = nc.tensor.matmul(bank(g), ut_hi[:, t], ht_lo[:, g * CH:(g + 1) * CH],
                                                start=False, stop=True)
                    last.then_inc(s_e, 1)

            def gather(t):
                if t == 0:
                    pe.wait_ge(s_hrc, NG * b + NG)
                pe.wait_ge(s_prob, T * b + t + 1)
                if t in SHARED:
                    pe.wait_ge(s_prob_dve, len(SHARED) * b + SHARED.index(t) + 1)
                pe.wait_ge(s_hnorm, T * b + t + 1)
                for g in range(G):
                    last = nc.tensor.matmul(ps_z[g], h_norm[t % 2][:], natural(prob[t % RINGC][:], g),
                                            start=t == 0, stop=t == T - 1)
                last.then_inc(s_pv, 1)

            for i in range(ROWS_BEFORE):
                rows_of_h(i)
            scores(0)
            for i in range(ROWS_BEFORE, NG):
                rows_of_h(i)
            scores(1)
            for t in range(T):
                if t + 2 < T:
                    scores(t + 2)
                gather(t)

        def pool_layers(pool, b, end, more):
            for u in range(NU):
                if ON_POOL[u]:
                    make_lo(pool, nc.gpsimd, b, u, s_lo_pool)
                if u in BIAS_AT:
                    g = BIAS_AT.index(u)
                    pool.wait_ge(s_xlo, L * T * b + (L - 1) * T + (g + 1) * TG)
                    h = feat[:, g * TG:(g + 1) * TG]
                    nc.gpsimd.tensor_tensor(h, h, bias[:, L - 1:L].broadcast_to([P, TG, P]), ALU.add).then_inc(s_hb, 1)

        def pool_attention(pool, b, more):
            for i, (t0, t1) in enumerate(GROUPS):
                pool.wait_ge(s_hrc, NG * b + i + 1)
                r = h_rows[:, t0:t1]
                nc.gpsimd.tensor_tensor(r, r, bias[:, L:L + 1].broadcast_to([P, t1 - t0, P]), ALU.add).then_inc(s_hrb, 1)
            for t in range(T):
                pool.wait_ge(s_exp, T * b + t + 1)
                cols = slice(0, HALF if t in SHARED else N)
                r = prob[t % RINGC][:, cols]
                nc.gpsimd.tensor_tensor(r, r, adj_t[:, t, cols], ALU.mult).then_inc(s_prob, 1)

        def graphs(eng, layers, attention, end):
            layers(eng, 0, False, True)
            with eng.Fori(0, B - 2) as b:
                attention(eng, b, True)
                layers(eng, b + 1, True, True)
            attention(eng, B - 2, True)
            layers(eng, B - 1, True, False)
            attention(eng, B - 1, False)
            if end is not None:
                end(eng, B - 1)

        block = ctx.enter_context(nc.Block())

        @block.sync
        def _(sp):
            for v in range(NV // FIRST // 2 + 1):
                load_first(sp, v)
            sp.dma_start(raw_ww[:], W_w).then_inc(s_const, 16)
            sp.dma_start(raw_a[:], A).then_inc(s_const, 16)
            for i, w in enumerate((W1, W2, W3)):
                sp.dma_start(w_sb[:, i], w).then_inc(s_const, 16)
            for i, row in enumerate(bias_in):
                sp.dma_start(bias[:, i], row.partition_broadcast(P)).then_inc(s_const, 16)
            sp.dma_start(wb_col[:, 0:1], W_b.rearrange("(p o) -> p o", o=1)).then_inc(s_const, 16)
            sp.dma_start(ww_g[:, P:W1G], gate_w[0:P]).then_inc(s_const, 16)
            sp.dma_start(ident_g[:, P:W1G], gate_w[P:2 * P]).then_inc(s_const, 16)
            sp.dma_start(gb[:], gate_b.partition_broadcast(P)).then_inc(s_const, 16)
            for v in range(NV // FIRST // 2 + 1, NV // FIRST):
                load_first(sp, v)
            sp.wait_ge(s_paired, NV // FIRST)
            load_x(sp, 0, 0)
            load_x(sp, 0, 1)
            graphs(sp, sync_layers, sync_attention, sync_end)

        @block.scalar
        def _(act):
            degree_root(act, 0)
            act.wait_ge(s_newton, NEWTON)
            nc.scalar.activation(dinv[:], newton[:], ACT.Copy).then_inc(s_dinv, 1)
            graphs(act, scalar_layers, scalar_attention, scalar_end)

        @block.gpsimd
        def _(pool):
            nc.gpsimd.memset(ones[:], 1.0).then_inc(s_ones, 1)
            nc.gpsimd.memset(ident, 0.0).then_inc(s_ident0, 1)
            pool.wait_ge(s_ident0, 1)
            nc.gpsimd.affine_select(out=ident, in_=ident, compare_op=ALU.not_equal, fill=1.0, base=0,
                                    pattern=[[-1, P]], channel_multiplier=1).then_inc(s_ident, 1)
            for v in range(NV // FIRST):
                t, rows = first_part(v)
                pool.wait_ge(s_turned, FIRST * (v + 1))
                if t > 0:
                    pool.wait_ge(s_paired, v - PER_J // FIRST + 1)
                nc.gpsimd.tensor_tensor(pair_sum[:, rows], adj_t[:, t, rows], adj_t[:, t + 1, rows],
                                        ALU.add).then_inc(s_pair, 1)
            graphs(pool, pool_layers, pool_attention, None)

        @block.vector
        def _(dve):
            for v in range(NV // FIRST):
                turn_first(dve, v)
                if v == WEIGHTS_V + 1:
                    dve.wait_ge(s_wt, 1)
                    nc.vector.tensor_copy(ww_t, bank(0)[:, 0:P]).then_inc(s_wc, 1)
                    nc.vector.tensor_tensor(a_sym[:], bank(0)[:, P:2 * P], raw_a[:], ALU.add).then_inc(s_sym, 1)
                if v == WEIGHTS_V + 2:
                    dve.wait_ge(s_sw, 1)
                    nc.vector.tensor_copy(sw_t[:], bank(1)[:, 0:P]).then_inc(s_swc, 1)
                    nc.vector.tensor_copy(wb_col[:, 1:2], bank(1)[:, P:P + 1]).then_inc(s_swc, 1)
            first_degrees(dve)
            for i in range(NEWTON):
                newton_step(dve, 0, i)
            graphs(dve, vector_layers, vector_attention, vector_end)

        @block.tensor
        def _(pe):
            def sum_part(v):
                t, rows = first_part(v)
                bank_z = ps_z[v % G]
                pe.wait_ge(s_turned, FIRST * (v + 1))
                for s in (2, 3):
                    nc.tensor.matmul(bank_z, ones[:], adj_t[:, t + s, rows], start=t == 0 and s == 2, stop=False)
                pe.wait_ge(s_pair, v + 1)
                nc.tensor.matmul(bank_z, ones[:], pair_sum[:, rows], start=False,
                                 stop=t == T - TG).then_inc(s_paired, 1)

            pe.wait_ge(s_ones, 1)
            for v in range(NV // FIRST):
                sum_part(v)
                if v == WEIGHTS_V:
                    pe.wait_ge(s_const, 16 * N_CONST)
                    pe.wait_ge(s_ident, 1)
                    nc.tensor.transpose(bank(0)[:, 0:P], raw_ww[:], ident)
                    nc.tensor.transpose(bank(0)[:, P:2 * P], raw_a[:], ident).then_inc(s_wt, 1)
                if v == WEIGHTS_V + 1:
                    pe.wait_ge(s_sym, 1)
                    nc.tensor.matmul(bank(1)[:, 0:P], raw_ww[:], a_sym[:], start=True, stop=True)
                    nc.tensor.matmul(bank(1)[:, P:P + 1], a_sym[:], wb_col[:, 0:1], start=True,
                                     stop=True).then_inc(s_sw, 1)
            pe.wait_ge(s_swc, 2)
            graphs(pe, tensor_layers, tensor_attention, tensor_end)


_INS = ["x", "adj", "L0_gnn_W1", "L0_gnn_b1", "L0_gnn_W2", "L0_gnn_b2", "L0_gnn_W3", "L0_gnn_b3",
        "L1_gnn_W_w", "L1_gnn_W_b", "L1_gnn_A", "L1_gnn_gate_w", "L1_gnn_gate_b"]


def kernel(**inputs):
    import numpy as _np
    import concourse.bacc as _bacc
    from concourse import mybir as _mybir
    from concourse.bass_utils import run_bass_kernel_spmd as _run

    nc = _bacc.Bacc("TRN2", target_bir_lowering=False, num_devices=1)
    arrays, args = {}, []
    for name in _INS:
        a = _np.ascontiguousarray(inputs[name])
        arrays[f"in_{name}_dram"] = a
        args.append(nc.dram_tensor(f"in_{name}_dram", a.shape, _mybir.dt.from_np(a.dtype), kind="ExternalInput").ap())
    shape = inputs["x"].shape
    args.append(nc.dram_tensor("out_0_dram", shape, _mybir.dt.float32, kind="ExternalOutput").ap())
    gnn_kernel(nc, *args)
    r = _run(nc, [arrays], core_ids=[0])
    return r.results[0]["out_0_dram"]
```
